# Optimizing a Trainium2 kernel written in Bass

```python
import numpy as np
import jax
import jax.numpy as jnp

def _softmax(x, axis=-1):
    return jax.nn.softmax(x, axis=axis)

def _gelu(x):
    return jax.nn.gelu(x, approximate=True)

def _silu(x):
    return jax.nn.silu(x)

def _sigmoid(x):
    return jax.nn.sigmoid(x)

def _layernorm(x, axis=-1, eps=1e-05):
    m = jnp.mean(x, axis=axis, keepdims=True)
    v = jnp.var(x, axis=axis, keepdims=True)
    return (x - m) / jnp.sqrt(v + eps)

def _scatter_add(tgt, idx, src, axis=0):
    return tgt.at[idx].add(src)

def _segment_sum(src, seg, n):
    return jax.ops.segment_sum(src, seg, n)
kernel_name = 'mk_vit_tower_cls_d1_tok_img512_r4_966690'

def setup_inputs(seed: int=0):
    np.random.seed(seed)
    _w = jnp.asarray

    def _rec_inputs():
        import jax
        import jax.numpy as jnp
        _rk = jax.random.key(seed)
        x = -0.000153849 + 1.00027 * jax.random.normal(jax.random.fold_in(_rk, 1), (8, 3, 224, 224), jnp.float32)
        cls_tok = 0.02 * jax.random.normal(jax.random.fold_in(_rk, 5), (1, 1, 128), jnp.float32)
        return (x, cls_tok)
    x, cls_tok = _rec_inputs()

    def _L0_tok_setup():
        import jax, jax.numpy as jnp
        import numpy as np
        PATCH = 4
        EMBED = 128
        BATCH = 32
        key = jax.random.key(seed)
        k1, k2, k3 = jax.random.split(key, 3)
        x = jax.random.normal(k1, (BATCH, 3, 64, 64), dtype=jnp.float32)
        W = jax.random.normal(k2, (EMBED, PATCH * PATCH * 3), dtype=jnp.float32) * 0.02
        b = jnp.zeros((EMBED,), dtype=jnp.float32)
        cls = jax.random.normal(k3, (1, 1, EMBED), dtype=jnp.float32)
        return {'x': x, 'W': W, 'b': b, 'cls': cls}
    _L0_tok_all = _L0_tok_setup()
    _L0_tok_in = {k: v for k, v in _L0_tok_all.items() if k in ('W', 'b', 'cls')}
    del _L0_tok_all

    def _L0_attn_setup():
        import jax, jax.numpy as jnp
        import numpy as np
        B, N, C = (2, 1024, 128)
        NUM_HEADS = 8
        HEAD_DIM = C // NUM_HEADS
        SCALE = HEAD_DIM ** (-0.5)
        THETA = 10000.0

        def _rope(x, seq_len, head_dim):
            freqs = 1.0 / THETA ** (jnp.arange(0, head_dim, 2, dtype=jnp.float32) / head_dim)
            t = jnp.arange(seq_len, dtype=jnp.float32)
            freqs_cis = jnp.outer(t, freqs)
            sin_f = jnp.sin(freqs_cis)
            cos_f = jnp.cos(freqs_cis)
            x_even = x[..., ::2]
            x_odd = x[..., 1::2]
            rot = jnp.stack([x_even * cos_f - x_odd * sin_f, x_even * sin_f + x_odd * cos_f], axis=-1)
            return rot.reshape(x.shape)
        key = jax.random.key(seed)
        ks = jax.random.split(key, 5)
        x = jax.random.normal(ks[0], (B, N, C), dtype=jnp.float32)
        Wqkv = jax.random.normal(ks[1], (3 * C, C), dtype=jnp.float32) * 0.02
        bqkv = jax.random.normal(ks[2], (3 * C,), dtype=jnp.float32) * 0.02
        Wproj = jax.random.normal(ks[3], (C, C), dtype=jnp.float32) * 0.02
        bproj = jax.random.normal(ks[4], (C,), dtype=jnp.float32) * 0.02
        return {'x': x, 'Wqkv': Wqkv, 'bqkv': bqkv, 'Wproj': Wproj, 'bproj': bproj}
    _L0_attn_all = _L0_attn_setup()
    _L0_attn_in = {k: v for k, v in _L0_attn_all.items() if k in ('Wqkv', 'bqkv', 'Wproj', 'bproj')}
    del _L0_attn_all

    def _L0_ffn_setup():
        import jax, jax.numpy as jnp
        import numpy as np
        B, S, D, E, O = (256, 64, 128, 16, 128)
        key = jax.random.key(seed)
        k_x, k_wg, k_bg, k_we, k_be = jax.random.split(key, 5)
        scale_g = 1.0 / np.sqrt(D)
        scale_e = 1.0 / np.sqrt(D)
        return {'x': jax.random.normal(k_x, (B, S, D), dtype=jnp.float32), 'Wg': jax.random.uniform(k_wg, (D, E), jnp.float32, -scale_g, scale_g), 'bg': jax.random.uniform(k_bg, (E,), jnp.float32, -scale_g, scale_g), 'We': jax.random.uniform(k_we, (E, D, O), jnp.float32, -scale_e, scale_e), 'be': jax.random.uniform(k_be, (E, O), jnp.float32, -scale_e, scale_e)}
    _L0_ffn_all = _L0_ffn_setup()
    _L0_ffn_in = {k: v for k, v in _L0_ffn_all.items() if k in ('Wg', 'bg', 'We', 'be')}
    del _L0_ffn_all
    return {'x': x, 'cls_tok': cls_tok, 'L0_tok_W': _L0_tok_in['W'], 'L0_tok_b': _L0_tok_in['b'], 'L0_tok_cls': _L0_tok_in['cls'], 'L0_attn_Wqkv': _L0_attn_in['Wqkv'], 'L0_attn_bqkv': _L0_attn_in['bqkv'], 'L0_attn_Wproj': _L0_attn_in['Wproj'], 'L0_attn_bproj': _L0_attn_in['bproj'], 'L0_ffn_Wg': _L0_ffn_in['Wg'], 'L0_ffn_bg': _L0_ffn_in['bg'], 'L0_ffn_We': _L0_ffn_in['We'], 'L0_ffn_be': _L0_ffn_in['be']}

def reference(x, cls_tok, L0_tok_W, L0_tok_b, L0_tok_cls, L0_attn_Wqkv, L0_attn_bqkv, L0_attn_Wproj, L0_attn_bproj, L0_ffn_Wg, L0_ffn_bg, L0_ffn_We, L0_ffn_be):
    import jax
    import jax.numpy as jnp

    def _L0_tok_ref(x, W, b, cls):
        import jax, jax.numpy as jnp
        import numpy as np
        PATCH = 4
        EMBED = 128
        BATCH = 32
        B, C, H, Wd = x.shape
        p = PATCH
        nh, nw = (H // p, Wd // p)
        patches = x.reshape(B, C, nh, p, nw, p)
        patches = patches.transpose(0, 2, 4, 1, 3, 5)
        patches = patches.reshape(B, nh * nw, C * p * p)
        proj = jnp.einsum('bld,ed->ble', patches, W) + b
        cls_tok = jnp.broadcast_to(cls, (B, 1, EMBED))
        return jnp.concatenate([cls_tok, proj], axis=1)

    def _L0_attn_ref(x, Wqkv, bqkv, Wproj, bproj):
        import jax, jax.numpy as jnp
        import numpy as np
        B, N, C = (2, 1024, 128)
        NUM_HEADS = 8
        HEAD_DIM = C // NUM_HEADS
        SCALE = HEAD_DIM ** (-0.5)
        THETA = 10000.0

        def _rope(x, seq_len, head_dim):
            freqs = 1.0 / THETA ** (jnp.arange(0, head_dim, 2, dtype=jnp.float32) / head_dim)
            t = jnp.arange(seq_len, dtype=jnp.float32)
            freqs_cis = jnp.outer(t, freqs)
            sin_f = jnp.sin(freqs_cis)
            cos_f = jnp.cos(freqs_cis)
            x_even = x[..., ::2]
            x_odd = x[..., 1::2]
            rot = jnp.stack([x_even * cos_f - x_odd * sin_f, x_even * sin_f + x_odd * cos_f], axis=-1)
            return rot.reshape(x.shape)
        b, n, c = x.shape
        qkv = x @ Wqkv.T + bqkv
        qkv = qkv.reshape(b, n, 3, NUM_HEADS, HEAD_DIM)
        qkv = jnp.transpose(qkv, (2, 0, 3, 1, 4))
        q, k, v = (qkv[0], qkv[1], qkv[2])
        q = _rope(q, n, HEAD_DIM)
        k = _rope(k, n, HEAD_DIM)
        attn = jnp.einsum('bhqd,bhkd->bhqk', q, k) * SCALE
        attn = jax.nn.softmax(attn, axis=-1)
        out = jnp.einsum('bhqk,bhkd->bhqd', attn, v)
        out = jnp.transpose(out, (0, 2, 1, 3)).reshape(b, n, c)
        return out @ Wproj.T + bproj

    def _L0_ffn_ref(x, Wg, bg, We, be):
        import jax, jax.numpy as jnp
        import numpy as np
        B, S, D, E, O = (256, 64, 128, 16, 128)
        scores = jax.nn.softmax(jnp.mean(x, axis=1) @ Wg + bg, axis=-1)
        idx = jnp.argmax(scores, axis=-1)
        gate = jnp.take_along_axis(scores, idx[:, None], axis=-1)
        W_sel = We[idx]
        b_sel = be[idx]
        y = jnp.einsum('bsd,bdo->bso', x, W_sel) + b_sel[:, None, :]
        return gate[:, :, None] * y
    h = _L0_tok_ref(x, L0_tok_W, L0_tok_b, L0_tok_cls)
    h = jnp.concatenate([jnp.broadcast_to(cls_tok, (h.shape[0], 1, h.shape[2])), h], axis=1)
    h = h + _L0_attn_ref(_layernorm(h, axis=-1), L0_attn_Wqkv, L0_attn_bqkv, L0_attn_Wproj, L0_attn_bproj)
    h = h + _L0_ffn_ref(_layernorm(h, axis=-1), L0_ffn_Wg, L0_ffn_bg, L0_ffn_We, L0_ffn_be)
    return h

_drawn_inputs = setup_inputs


def setup_inputs(seed=0):
    import zlib

    import numpy as np

    out = dict(_drawn_inputs(seed))
    spreads = {'L0_tok_b': (0.0, 0.1)}
    factors = {'cls_tok': 24.83}
    for name, (base, spread) in spreads.items():
        noise = np.random.default_rng([zlib.crc32(name.encode()), seed]).standard_normal(out[name].shape)
        drawn = base * np.exp(spread * noise) if base else spread * noise
        out[name] = jnp.asarray(drawn.astype(out[name].dtype))
    for name, factor in factors.items():
        out[name] = (out[name] * factor).astype(out[name].dtype)
    return out
```

```python
from contextlib import ExitStack

import concourse.bass as bass
from concourse import mybir

F32 = mybir.dt.float32
BF16 = mybir.dt.bfloat16
U32 = mybir.dt.uint32
ALU = mybir.AluOpType
ACT = mybir.ActivationFunctionType
AX = mybir.AxisListType
ds = bass.ds

B = 8
IMG, PATCH = 224, 4
GRID = IMG // PATCH
NP_ = GRID * GRID
N = NP_ + 2
C = 128
FEAT = 3 * PATCH * PATCH
HEADS, HD = 8, 16
GH = B * HEADS
EXPERTS = 16
P = 128
NT = -(-N // P)
LAST = N - P * (NT - 1)
GROUPS = [(g, min(4, NT - 4 * g)) for g in range(-(-NT // 4))]
NG = len(GROUPS)
EPS = 1e-5
SCALE = HD ** -0.5
THETA = 10000.0

CW = 448
NC = N // CW
CHUNKS = [(c * CW, CW if c < NC - 1 else N - CW * (NC - 1)) for c in range(NC)]
CMAX = CHUNKS[-1][1]

UNITS = [(0, 512, 2, 256), (1024, 512, 2, 256), (N - 1092, 364, 3, 273)]
NU = len(UNITS)
UMAX = 1092
OFF = [0, 256, 512]
OW = 512 + 273
UPH = NU * NT

Q_ROWS = [0, 1, 2, 0, 1, 0]
K_ROWS = [0, 0, 0, 1, 1, 2]
PAIRS = len(Q_ROWS)
KR = PAIRS * HD
SHIFT_ROWS = 2
KS = KR + SHIFT_ROWS
NSH = NT * P

SAFE = 60.0


def wait_apart(engine, sem, count, passed):
    engine.wait_ge(sem, count)
    engine.sem_inc(passed, 1)


def phase_embed_qkv(nc, io, scr, flag):
    ctx = ExitStack()
    with ctx:
        def sb(name, shape, dt=F32):
            return ctx.enter_context(nc.sbuf_tensor(name, shape, dt))

        def pb(name, shape):
            return ctx.enter_context(nc.psum_tensor(name, shape, F32))

        def sem(name):
            return ctx.enter_context(nc.semaphore(name))

        XS = sb("XS", [3 + FEAT, N])
        WE = sb("WE", [3 + FEAT, C])
        WQK = sb("WQK", [C, 4, C])
        BQK = sb("BQK", [C, 4])
        WV = sb("WV", [C, C])
        BV = sb("BV", [P, C])
        WROW = sb("WROW", [C, 2, C])
        HSUM = sb("HSUM", [C, HEADS])
        COS = sb("COS", [C, N])
        SIN = sb("SIN", [C, N])
        ident = sb("ident", [P, P])
        H = sb("H", [P, NT, C])
        STATS = sb("STATS", [P, NT, 6])
        MV = sb("MV", [P, NT, 2])
        STD = sb("STD", [P, NT])
        RSTD = sb("RSTD", [P, NT])
        XN = sb("XN", [P, NT, C])
        XNT = sb("XNT", [C, N])
        V = sb("V", [P, HEADS, NT, HD])
        T1 = sb("T1", [C, 2, CMAX])
        T2 = sb("T2", [C, 2, CMAX])
        QF = sb("QF", [C, 2, CMAX])
        RF = sb("RF", [C, 2, CMAX])
        PARTS = sb("PARTS", [C, 2, 3, N], BF16)
        sq = sb("sq", [C, 2, C])
        ss = sb("ss", [C, 2])
        nrm = sb("nrm", [C, 2])
        ab = sb("ab", [C, 2])
        bound = sb("bound", [C, 4])
        hq = sb("hq", [1, 3 * HEADS])
        zsh = sb("zsh", [P, 2 * NSH // 2], BF16)

        emb_ps = pb("emb_ps", [P, 2, 512])
        tr_ps = pb("tr_ps", [P, 2, 512])
        vqk_ps = pb("vqk_ps", [P, 2, 2, 512])

        weights_in = sem("weights_in")
        patches_in = sem("patches_in")
        consts_set = sem("consts_set")
        cls_cleared = sem("cls_cleared")
        embedded = sem("embedded")
        h_ready = sem("h_ready")
        stats_done = sem("stats_done")
        std_done = sem("std_done")
        rstd_done = sem("rstd_done")
        xn_ready = sem("xn_ready")
        transposed = sem("transposed")
        xnt_ready = sem("xnt_ready")
        vqk_done = sem("vqk_done")
        vqk_free = sem("vqk_free")
        t_done = sem("t_done")
        q_ready = sem("q_ready")
        hi_done = sem("hi_done")
        r_done = sem("r_done")
        mid_done = sem("mid_done")
        lo_done = sem("lo_done")
        h_stored = sem("h_stored")
        v_stored = sem("v_stored")
        qk_stored = sem("qk_stored")
        passed = sem("a_passed")
        b_step = sem("b_step")
        shift_in = sem("shift_in")
        block = ctx.enter_context(nc.Block())

        VUSES = -(-NG // 2)
        USES = VUSES + 2 * NC

        @block.sync
        def _(sp):
            sp.sem_inc(xnt_ready, 1)
            sp.sem_inc(h_ready, 1)
            sp.sem_inc(vqk_free, 2)
            sp.sem_inc(r_done, 2)
            sp.sem_inc(lo_done, 2)
            sp.sem_inc(h_stored, 16)
            sp.sem_inc(v_stored, 16)
            sp.sem_inc(qk_stored, 6 * 16)
            sp.wait_ge(cls_cleared, 1)
            sp.dma_start(XS[0:3, :], io["indicators"]).then_inc(weights_in, 16)
            sp.dma_start(WE[0:3 + FEAT, :], io["w_embed"]).then_inc(weights_in, 16)
            sp.dma_start(XS[3:3 + FEAT, 2:N], io["patches"][0]).then_inc(patches_in, 16)
            sp.dma_start(ident[:], io["ident"]).then_inc(weights_in, 16)
            sp.dma_start(WV[:], io["w_v"]).then_inc(weights_in, 16)
            sp.dma_start(BV[:], io["b_v"].partition_broadcast(P)).then_inc(weights_in, 16)
            sp.dma_start(WQK[:], io["w_qk"]).then_inc(weights_in, 16)
            sp.dma_start(BQK[:], io["b_qk"]).then_inc(weights_in, 16)
            sp.dma_start(COS[:], io["cos"]).then_inc(weights_in, 16)
            sp.dma_start(SIN[:], io["sin"]).then_inc(weights_in, 16)
            sp.dma_start(WROW[:], io["w_row"]).then_inc(weights_in, 16)
            sp.dma_start(HSUM[:], io["head_sum"]).then_inc(weights_in, 16)
            sp.wait_ge(consts_set, 2)
            sp.dma_start(scr["shift"].rearrange("g r n -> (g r n)").rearrange("(p f) -> p f", p=P),
                         zsh[:]).then_inc(shift_in, 16)

            def store(b):
                sp.wait_ge(h_ready, NG * b + NG + 1)
                sp.dma_start(scr["h"][b], H[:]).then_inc(h_stored, 16)
                sp.wait_ge(vqk_free, USES * b + VUSES + 2)
                sp.dma_start(scr["v"][b], V[:]).then_inc(v_stored, 16)
                for side in range(2):
                    sp.wait_ge(lo_done, 2 * NC * b + NC * (side + 1) + 2)
                    for part in range(3):
                        sp.dma_start(scr["qk"][b, side, part], PARTS[:, side, part, :]).then_inc(qk_stored, 16)

            with sp.Fori(0, B - 1) as b:
                sp.wait_ge(embedded, NG * b + NG)
                sp.dma_start(XS[3:3 + FEAT, 2:N], io["patches"][b + 1]).then_inc(patches_in, 16)
                store(b)
            store(B - 1)
            sp.wait_ge(h_stored, 16 * (B + 1))
            sp.wait_ge(v_stored, 16 * (B + 1))
            sp.wait_ge(qk_stored, 6 * 16 * (B + 1))
            sp.wait_ge(shift_in, 16)

        @block.gpsimd
        def _(pool):
            nc.gpsimd.memset(XS[:, 0:2], 0.0).then_inc(cls_cleared, 1)
            nc.gpsimd.memset(V[:], 0.0).then_inc(consts_set, 1)
            nc.gpsimd.memset(zsh[:], 0.0).then_inc(consts_set, 1)
            with pool.Fori(0, B) as b:
                for i in range(2 * NC + 1):
                    if i < 2 * NC:
                        side, (s, w) = i // NC, CHUNKS[i % NC]
                        pool.wait_ge(hi_done, 2 * NC * b + i + 1)
                        pool.wait_ge(lo_done, 2 * NC * b + i + 1)
                        nc.gpsimd.tensor_tensor(RF[:, i % 2, 0:w], QF[:, i % 2, 0:w],
                                                PARTS[:, side, 0, s:s + w], ALU.subtract).then_inc(r_done, 1)
                    if i >= 1:
                        j = i - 1
                        side, (s, w) = j // NC, CHUNKS[j % NC]
                        pool.wait_ge(mid_done, 2 * NC * b + j + 1)
                        nc.gpsimd.tensor_tensor(PARTS[:, side, 2, s:s + w], RF[:, j % 2, 0:w],
                                                PARTS[:, side, 1, s:s + w], ALU.subtract).then_inc(lo_done, 1)

        @block.scalar
        def _(act):
            act.wait_ge(weights_in, 11 * 16)
            nc.scalar.activation(sq[:, 0, :], WROW[:, 0, :], ACT.Square, accum_out=ss[:, 0:1]).then_inc(b_step, 1)
            nc.scalar.activation(sq[:, 1, :], WROW[:, 1, :], ACT.Square, accum_out=ss[:, 1:2]).then_inc(b_step, 1)
            nc.scalar.activation(ab[:], BQK[:, 0:3:2], ACT.Abs).then_inc(b_step, 1)
            act.wait_ge(b_step, 3)
            nc.scalar.activation(nrm[:], ss[:], ACT.Sqrt, scale=float(C)).then_inc(b_step, 1)
            with act.Fori(0, B) as b:
                act.wait_ge(h_stored, 16 * b + 16)
                for g, n in GROUPS:
                    rows = LAST if g == NG - 1 else P
                    act.wait_ge(embedded, NG * b + g + 1)
                    if g == 0:
                        act.wait_ge(xn_ready, NG * b + 1)
                    nc.scalar.activation(H[0:rows, 4 * g:4 * g + n, :],
                                         emb_ps[0:rows, g % 2, 0:n * C].rearrange("p (t c) -> p t c", c=C),
                                         ACT.Copy).then_inc(h_ready, 1)
                act.wait_ge(stats_done, 3 * b + 3)
                nc.scalar.activation(STD[:], MV[:, :, 1], ACT.Sqrt).then_inc(std_done, 1)
                for g, n in GROUPS:
                    rows = LAST if g == NG - 1 else n * P
                    act.wait_ge(transposed, NG * b + g + 1)
                    if g == 0:
                        act.wait_ge(vqk_done, USES * b + 1)
                    nc.scalar.activation(XNT[:, 4 * g * P:4 * g * P + rows], tr_ps[:, g % 2, 0:rows],
                                         ACT.Copy).then_inc(xnt_ready, 1)
                act.wait_ge(qk_stored, 6 * 16 * b + 6 * 16)
                for i in range(2 * NC + 1):
                    if i < 2 * NC:
                        side, (s, w) = i // NC, CHUNKS[i % NC]
                        act.wait_ge(q_ready, 2 * NC * b + i + 1)
                        nc.scalar.activation(PARTS[:, side, 0, s:s + w], QF[:, i % 2, 0:w],
                                             ACT.Copy).then_inc(hi_done, 1)
                    if i >= 1:
                        j = i - 1
                        side, (s, w) = j // NC, CHUNKS[j % NC]
                        act.wait_ge(r_done, 2 * NC * b + j + 3)
                        nc.scalar.activation(PARTS[:, side, 1, s:s + w], RF[:, j % 2, 0:w],
                                             ACT.Copy).then_inc(mid_done, 1)

        @block.vector
        def _(dve):
            nc.vector.memset(H[:, NT - 1, :], 0.0)
            nc.vector.memset(MV[:], 1.0).then_inc(xn_ready, 1)
            dve.wait_ge(b_step, 4)
            dve.wait_ge(xn_ready, 1)
            nc.vector.tensor_tensor(bound[:, 0:2], nrm[:], ab[:], ALU.add).then_inc(b_step, 1)
            dve.wait_ge(b_step, 5)
            nc.vector.tensor_tensor(bound[:, 2:4], bound[:, 0:2], bound[:, 0:2], ALU.mult).then_inc(b_step, 1)
            dve.wait_ge(b_step, 7)
            nc.vector.tensor_copy(hq[:, 0:2 * HEADS], emb_ps[0:1, 0, 0:2 * HEADS]).then_inc(b_step, 1)
            dve.wait_ge(b_step, 8)
            nc.vector.tensor_tensor(hq[:, 2 * HEADS:], hq[:, 0:HEADS], hq[:, HEADS:2 * HEADS],
                                    ALU.mult).then_inc(b_step, 1)
            dve.wait_ge(b_step, 9)
            nc.vector.tensor_reduce(hq[:, 0:1], hq[:, 2 * HEADS:], AX.X, ALU.max).then_inc(b_step, 1)
            dve.wait_ge(b_step, 10)
            nc.vector.tensor_scalar(flag[:], hq[:, 0:1], (SAFE / SCALE) ** 2, None, ALU.is_gt).then_inc(b_step, 1)
            with dve.Fori(0, B) as b:
                for g, n in GROUPS:
                    dve.wait_ge(h_ready, NG * b + g + 2)
                    for t in range(4 * g, 4 * g + n):
                        rows = LAST if t == NT - 1 else P
                        last = nc.vector.bn_stats(STATS[0:rows, t, :], H[0:rows, t, :])
                last.then_inc(stats_done, 1)
                wait_apart(dve, stats_done, 3 * b + 1, passed)
                for t in range(NT):
                    rows = LAST if t == NT - 1 else P
                    last = nc.vector.bn_aggr(MV[0:rows, t, :], STATS[0:rows, t, :])
                last.then_inc(stats_done, 1)
                dve.wait_ge(stats_done, 3 * b + 2)
                nc.vector.tensor_scalar(MV[:, :, 1], MV[:, :, 1], EPS, None, ALU.add).then_inc(stats_done, 1)
                dve.wait_ge(std_done, b + 1)
                nc.vector.reciprocal(RSTD[:], STD[:]).then_inc(rstd_done, 1)
                dve.wait_ge(rstd_done, b + 1)
                for g, n in GROUPS:
                    for t in range(4 * g, 4 * g + n):
                        rows = LAST if t == NT - 1 else P
                        last = nc.vector.tensor_scalar(XN[0:rows, t, :], H[0:rows, t, :], MV[0:rows, t, 0:1],
                                                       RSTD[0:rows, t:t + 1], ALU.subtract, ALU.mult)
                    last.then_inc(xn_ready, 1)
                dve.wait_ge(v_stored, 16 * b + 16)
                dve.wait_ge(consts_set, 2)
                for i in range(VUSES):
                    t0, t1 = 8 * i, min(8 * i + 8, NT)
                    rows = LAST if t1 == NT else P
                    dve.wait_ge(vqk_done, USES * b + i + 2)
                    last = nc.vector.tensor_tensor(
                        V[0:rows, :, t0:t1, :].rearrange("p h t d -> p t h d"),
                        vqk_ps[0:rows, i % 2, :, :].rearrange("p a (t h d) -> p (a t) h d", h=HEADS, d=HD)[:, 0:t1 - t0],
                        BV[0:rows, :].rearrange("p (h d) -> p h d", d=HD)[:, None].to_broadcast(
                            [rows, t1 - t0, HEADS, HD]) if t1 - t0 > 1 else
                        BV[0:rows, :].rearrange("p (h d) -> p h d", d=HD)[:, None],
                        ALU.add).then_inc(vqk_free, 1)
                for i in range(2 * NC):
                    side, (s, w) = i // NC, CHUNKS[i % NC]
                    u = VUSES + i
                    dve.wait_ge(vqk_done, USES * b + u + 2)
                    dve.wait_ge(q_ready, 2 * NC * b + i) if i else None
                    nc.vector.scalar_tensor_tensor(T1[:, i % 2, 0:w], vqk_ps[:, u % 2, 0, 0:w],
                                                   BQK[:, 2 * side:2 * side + 1], COS[:, s:s + w],
                                                   ALU.add, ALU.mult)
                    nc.vector.scalar_tensor_tensor(T2[:, i % 2, 0:w], vqk_ps[:, u % 2, 1, 0:w],
                                                   BQK[:, 2 * side + 1:2 * side + 2], SIN[:, s:s + w],
                                                   ALU.add, ALU.mult).then_inc(vqk_free, 1)
                    dve.wait_ge(vqk_free, USES * b + u + 3)
                    dve.wait_ge(r_done, 2 * NC * b + i + 1)
                    nc.vector.tensor_tensor(QF[:, i % 2, 0:w], T1[:, i % 2, 0:w], T2[:, i % 2, 0:w],
                                            ALU.add).then_inc(q_ready, 1)

        @block.tensor
        def _(pe):
            pe.wait_ge(weights_in, 11 * 16)
            pe.wait_ge(b_step, 6)
            for side in range(2):
                nc.tensor.matmul(emb_ps[0:1, 0, side * HEADS:(side + 1) * HEADS], bound[:, 2 + side:3 + side],
                                 HSUM[:], start=True, stop=True).then_inc(b_step, 1) if side else \
                    nc.tensor.matmul(emb_ps[0:1, 0, 0:HEADS], bound[:, 2:3], HSUM[:], start=True, stop=True)
            pe.wait_ge(b_step, 8)
            nc.tensor.matmul(vqk_ps[0:1, 0, 0, 0:HEADS], bound[:, 2:3], HSUM[:], start=True,
                             stop=True).then_inc(vqk_done, 1)
            with pe.Fori(0, B) as b:
                pe.wait_ge(patches_in, 16 * b + 16)
                for g, n in GROUPS:
                    pe.wait_ge(h_ready, NG * b + 1 + max(g - 1, 0))
                    for t in range(4 * g, 4 * g + n):
                        rows = LAST if t == NT - 1 else P
                        last = nc.tensor.matmul(emb_ps[0:rows, g % 2, (t % 4) * C:(t % 4 + 1) * C],
                                                XS[:, t * P:t * P + rows], WE[:], start=True, stop=True)
                    last.then_inc(embedded, 1)
                for g, n in GROUPS:
                    pe.wait_ge(xn_ready, NG * b + g + 2)
                    pe.wait_ge(xnt_ready, NG * b + 1 + max(g - 1, 0))
                    for t in range(4 * g, 4 * g + n):
                        rows = LAST if t == NT - 1 else P
                        last = nc.tensor.transpose(tr_ps[:, g % 2, (t % 4) * P:(t % 4) * P + rows],
                                                   XN[0:rows, t, :], ident[0:rows, 0:rows])
                    last.then_inc(transposed, 1)
                pe.wait_ge(xnt_ready, NG * b + NG + 1)
                for i in range(VUSES):
                    pe.wait_ge(vqk_free, USES * b + i + 1)
                    for t in range(8 * i, min(8 * i + 8, NT)):
                        rows = LAST if t == NT - 1 else P
                        last = nc.tensor.matmul(vqk_ps[0:rows, i % 2, t % 8 // 4, (t % 4) * C:(t % 4 + 1) * C],
                                                XNT[:, t * P:t * P + rows], WV[:], start=True, stop=True)
                    last.then_inc(vqk_done, 1)
                for i in range(2 * NC):
                    side, (s, w) = i // NC, CHUNKS[i % NC]
                    u = VUSES + i
                    pe.wait_ge(vqk_free, USES * b + u + 1)
                    for a in range(2):
                        last = nc.tensor.matmul(vqk_ps[:, u % 2, a, 0:w], WQK[:, 2 * side + a, :],
                                                XNT[:, s:s + w], start=True, stop=True)
                    last.then_inc(vqk_done, 1)


def phase_maxima(nc, scr, flag):
    ctx = ExitStack()
    with ctx:
        KM = ctx.enter_context(nc.sbuf_tensor("KM", [KR, N], BF16))
        QM = ctx.enter_context(nc.sbuf_tensor("QM", [KR, N], BF16))
        MX = ctx.enter_context(nc.sbuf_tensor("MX", [P, NT], F32))
        NM = ctx.enter_context(nc.sbuf_tensor("NM", [P, NT], F32))
        NHL = ctx.enter_context(nc.sbuf_tensor("NHL", [P, SHIFT_ROWS, NT], BF16))
        mx_ps = ctx.enter_context(nc.psum_tensor("mx_ps", [P, 7, 512], F32))
        loaded = ctx.enter_context(nc.semaphore("m_loaded"))
        scored = ctx.enter_context(nc.semaphore("m_scored"))
        reduced = ctx.enter_context(nc.semaphore("m_reduced"))
        passed = ctx.enter_context(nc.semaphore("m_passed"))
        split = ctx.enter_context(nc.semaphore("m_split"))
        stored = ctx.enter_context(nc.semaphore("m_stored"))
        block = ctx.enter_context(nc.Block())
        W = 449
        starts = [min(c * 448, N - W) for c in range(7)]

        @block.sync
        def _(sp):
            needed = sp.value_load(flag[0:1, 0:1], min_val=0, max_val=1)
            with sp.If(needed > 0):
                sp.sem_inc(reduced, 1)
                sp.sem_inc(stored, 32)
                with sp.Fori(0, GH) as g:
                    sp.wait_ge(reduced, NT * g + 1)
                    for i in range(PAIRS):
                        sp.dma_start(QM[i * HD:(i + 1) * HD, :], scr["qk_head"](g, 0, Q_ROWS[i])).then_inc(loaded, 16)
                        sp.dma_start(KM[i * HD:(i + 1) * HD, :], scr["qk_head"](g, 1, K_ROWS[i])).then_inc(loaded, 16)
                    sp.wait_ge(split, 3 * g + 3)
                    with nc.allow_non_contiguous_dma(reason="a column of maxima becomes a row"):
                        for r in range(SHIFT_ROWS):
                            sp.dma_start(scr["shift"][g, r, :].rearrange("(t p) -> p t", p=P),
                                         NHL[:, r, :]).then_inc(stored, 16)
                sp.wait_ge(stored, 32 * (GH + 1))

        @block.tensor
        def _(pe):
            needed = pe.value_load(flag[0:1, 0:1], min_val=0, max_val=1)
            with pe.If(needed > 0):
                with pe.Fori(0, GH) as g:
                    wait_apart(pe, loaded, 2 * PAIRS * 16 * g + 2 * PAIRS * 16, passed)
                    with pe.Fori(0, NT - 1) as t:
                        pe.wait_ge(reduced, NT * g + t + 1)
                        for c in range(7):
                            last = nc.tensor.matmul(mx_ps[:, c, 0:W], QM[:, ds(t * P, P)],
                                                    KM[:, starts[c]:starts[c] + W], start=True, stop=True)
                        last.then_inc(scored, 1)
                    pe.wait_ge(reduced, NT * g + NT)
                    for c in range(7):
                        last = nc.tensor.matmul(mx_ps[0:LAST, c, 0:W], QM[:, N - LAST:N],
                                                KM[:, starts[c]:starts[c] + W], start=True, stop=True)
                    last.then_inc(scored, 1)

        @block.vector
        def _(dve):
            needed = dve.value_load(flag[0:1, 0:1], min_val=0, max_val=1)
            with dve.If(needed > 0):
                nc.vector.memset(MX[:], 0.0)
                with dve.Fori(0, GH) as g:
                    with dve.Fori(0, NT - 1) as t:
                        dve.wait_ge(scored, NT * g + t + 1)
                        nc.vector.tensor_reduce(MX[:, ds(t, 1)], mx_ps[:, :, 0:W], AX.XY,
                                                ALU.max).then_inc(reduced, 1)
                    dve.wait_ge(scored, NT * g + NT)
                    nc.vector.tensor_reduce(MX[0:LAST, NT - 1:NT], mx_ps[0:LAST, :, 0:W], AX.XY,
                                            ALU.max).then_inc(reduced, 1)
                    dve.wait_ge(reduced, NT * g + NT + 1)
                    dve.wait_ge(stored, 32 * g + 32)
                    nc.vector.tensor_scalar(NM[:], MX[:], -1.0, None, ALU.mult).then_inc(split, 1)
                    dve.wait_ge(split, 3 * g + 1)
                    nc.vector.tensor_copy(NHL[:, 0, :], NM[:]).then_inc(split, 1)
                    dve.wait_ge(split, 3 * g + 2)
                    nc.vector.tensor_tensor(NHL[:, 1, :], NM[:], NHL[:, 0, :], ALU.subtract).then_inc(split, 1)


def phase_attention(nc, scr):
    ctx = ExitStack()
    with ctx:
        def sb(name, shape, dt=F32):
            return ctx.enter_context(nc.sbuf_tensor(name, shape, dt))

        def sem(name):
            return ctx.enter_context(nc.semaphore(name))

        KA = [sb(f"KA{i}", [KS, N], BF16) for i in range(2)]
        QA = [sb(f"QA{i}", [KS, N], BF16) for i in range(2)]
        VH = [sb(f"VH{i}", [P, NT, HD]) for i in range(2)]
        VST = [sb(f"VST{i}", [P, 2 * HD]) for i in range(2)]
        E = [sb(f"E{u}", [P, UMAX]) for u in range(NU)]
        OB = [sb(f"OB{i}", [P, OW]) for i in range(2)]
        S = [ctx.enter_context(nc.psum_tensor(f"S{i}", [P, 3, 512], F32)) for i in range(2)]
        PO = [ctx.enter_context(nc.psum_tensor(f"PO{i}", [P, 512], F32)) for i in range(2)]

        passed = sem("b_passed")
        consts = sem("a_consts")
        exp_loaded = sem("exp_loaded")
        qk_in = [sem(f"qk_in{i}") for i in range(2)]
        v_in = [sem(f"v_in{i}") for i in range(2)]
        scores = sem("scores")
        probs = sem("probs")
        used = sem("used")
        v_staged = sem("v_staged")
        o_out = [sem(f"o_out{i}") for i in range(2)]
        o_stored = [sem(f"o_stored{i}") for i in range(2)]
        block = ctx.enter_context(nc.Block())
        LOADS = 2 * PAIRS + 1

        @block.sync
        def _(sp):
            sp.sem_inc(used, 4)
            sp.sem_inc(o_out[0], 1)
            sp.sem_inc(o_out[1], 1)

            def load(g, par):
                for i in range(PAIRS):
                    sp.dma_start(QA[par][i * HD:(i + 1) * HD, :], scr["qk_head"](g, 0, Q_ROWS[i])).then_inc(qk_in[par], 16)
                    sp.dma_start(KA[par][i * HD:(i + 1) * HD, :], scr["qk_head"](g, 1, K_ROWS[i])).then_inc(qk_in[par], 16)
                sp.dma_start(QA[par][KR:KS, :], scr["shift"][g, :, 0:N]).then_inc(qk_in[par], 16)
                sp.dma_start(VH[par][:], scr["v_head"](g)).then_inc(v_in[par], 16)

            def store(g, par):
                sp.wait_ge(o_out[0], g + 2)
                sp.wait_ge(o_out[1], g + 2)
                sp.dma_start(scr["o"][g], OB[par][:]).then_inc(o_stored[par], 16)

            load(0, 0)
            load(1, 1)
            with sp.Fori(1, GH // 2) as pair:
                for par in range(2):
                    g = 2 * pair + par
                    sp.wait_ge(scores, UPH * g - UPH)
                    sp.wait_ge(v_staged, NT * g - NT)
                    load(g, par)
                    store(g - 2, par)
            for par in range(2):
                store(GH - 2 + par, par)
            for par in range(2):
                sp.wait_ge(o_stored[par], 16 * (GH // 2))

        @block.gpsimd
        def _(pool):
            for i in range(2):
                nc.gpsimd.memset(VST[i][:, HD:], 1.0).then_inc(consts, 1)

            def stage(gk, par, kt, slot):
                wait_apart(pool, used, NU * gk + 1, passed)
                nc.gpsimd.tensor_copy(VST[slot][:, 0:HD], VH[par][:, kt, :] if isinstance(kt, int) else
                                      VH[par][:, ds(kt, 1), :].rearrange("p a d -> p (a d)")).then_inc(v_staged, 1)

            with pool.Fori(0, GH // 2) as pair:
                for par in range(2):
                    g = 2 * pair + par
                    wait_apart(pool, v_in[par], 16 * pair + 16, passed)
                    with pool.Fori(0, NT // 2) as half:
                        for k in range(2):
                            stage(NT * g + 2 * half + k, par, 2 * half + k, (par + k) % 2)
                    stage(NT * g + NT - 1, par, NT - 1, (par + NT - 1) % 2)

        @block.vector
        def _(dve):
            for i in range(2):
                nc.vector.memset(KA[i][KR:KS, :], 1.0).then_inc(consts, 1)

            def copy_out(g, par):
                dve.wait_ge(used, UPH * g + UPH - 1 + 4)
                nc.vector.tensor_copy(OB[par][:, 0:512], PO[0][:]).then_inc(o_out[0], 1)
                dve.wait_ge(used, UPH * g + UPH + 4)
                nc.vector.tensor_copy(OB[par][:, 512:OW], PO[1][:, 0:OW - 512]).then_inc(o_out[1], 1)

            dve.wait_ge(exp_loaded, 1)
            for par in range(2):
                copy_out(par, par)
            with dve.Fori(1, GH // 2) as pair:
                for par in range(2):
                    dve.wait_ge(o_stored[par], 16 * pair)
                    copy_out(2 * pair + par, par)

        @block.scalar
        def _(act):
            def exp_tile(g, par, kt, ktp, rows):
                for u, (_, w, n, _) in enumerate(UNITS):
                    unit = UPH * g + NU * kt + u
                    act.wait_ge(scores, unit + 1)
                    act.wait_ge(used, unit + 2)
                    nc.scalar.activation(E[u][0:rows, 0:n * w].rearrange("p (n w) -> p n w", w=w),
                                         S[(par + ktp + u) % 2][0:rows, 0:n, 0:w], ACT.Exp,
                                         scale=SCALE).then_inc(probs, 1)

            act.wait_ge(consts, 4)
            nc.scalar.activation(OB[0][0:1, 0:1], VST[0][0:1, HD:HD + 1], ACT.Exp).then_inc(exp_loaded, 1)
            with act.Fori(0, GH // 2) as pair:
                for par in range(2):
                    g = 2 * pair + par
                    with act.Fori(0, NT // 2) as half:
                        for k in range(2):
                            exp_tile(g, par, 2 * half + k, k, P)
                    exp_tile(g, par, NT - 1, 0, LAST)

        @block.tensor
        def _(pe):
            def qk(g, par, kt, ktp, u, wait=True):
                q0, w, n, _ = UNITS[u]
                rows = LAST if isinstance(kt, int) and kt == NT - 1 else P
                keys = KA[par][:, kt * P:kt * P + rows] if isinstance(kt, int) else KA[par][:, ds(kt * P, P)]
                if wait:
                    pe.wait_ge(probs, UPH * g + NU * kt + u - 1)
                for j in range(n):
                    last = nc.tensor.matmul(S[(par + ktp + u) % 2][0:rows, j, 0:w], keys,
                                            QA[par][:, q0 + j * w:q0 + (j + 1) * w], start=True, stop=True)
                last.then_inc(scores, 1)

            def pv(g, par, kt, ktp, u):
                first = isinstance(kt, int) and kt == 0
                rows = LAST if isinstance(kt, int) and kt == NT - 1 else P
                pw = UNITS[u][3]
                bank, at = OFF[u] // 512, OFF[u] % 512
                pe.wait_ge(probs, UPH * g + NU * kt + u + 1)
                if u == 0:
                    pe.wait_ge(v_staged, NT * g + kt + 1)
                if first and u != 1:
                    pe.wait_ge(o_out[bank], g + 1)
                for j in range(4):
                    last = nc.tensor.matmul(PO[bank][32 * j:32 * j + 32, at:at + pw],
                                            VST[(par + ktp) % 2][0:rows, :], E[u][0:rows, j * pw:(j + 1) * pw],
                                            start=first and u != 1,
                                            stop=isinstance(kt, int) and kt == NT - 1,
                                            skip_group_check=True)
                last.then_inc(used, 1)

            def first_scores(g, par, pair, u, wait=True):
                if u == 0:
                    pe.wait_ge(qk_in[par], 16 * LOADS * pair + 16 * LOADS)
                qk(g, par, 0, 0, u, wait)

            def head(g, par, nxt):
                qk(g, par, 0, 0, 2)
                pv(g, par, 0, 0, 0)

                def step(kt, ktp, prev):
                    qk(g, par, kt, ktp, 0)
                    pv(g, par, prev, (ktp + 1) % 2, 1)
                    qk(g, par, kt, ktp, 1)
                    pv(g, par, prev, (ktp + 1) % 2, 2)
                    qk(g, par, kt, ktp, 2)
                    pv(g, par, kt, ktp, 0)

                step(1, 1, 0)
                with pe.Fori(1, NT // 2) as half:
                    step(2 * half, 0, 2 * half - 1)
                    step(2 * half + 1, 1, 2 * half)
                step(NT - 1, 0, NT - 2)
                if nxt is not None:
                    first_scores(*nxt, 0)
                pv(g, par, NT - 1, 0, 1)
                if nxt is not None:
                    first_scores(*nxt, 1)
                pv(g, par, NT - 1, 0, 2)

            pe.wait_ge(consts, 4)
            first_scores(0, 0, 0, 0, wait=False)
            first_scores(0, 0, 0, 1, wait=False)
            with pe.Fori(0, GH // 2 - 1) as pair:
                head(2 * pair, 0, (2 * pair + 1, 1, pair))
                head(2 * pair + 1, 1, (2 * pair + 2, 0, pair + 1))
            head(GH - 2, 0, (GH - 1, 1, GH // 2 - 1))
            head(GH - 1, 1, None)


def phase_project_ffn(nc, io, scr, out):
    ctx = ExitStack()
    with ctx:
        def sb(name, shape, dt=F32):
            return ctx.enter_context(nc.sbuf_tensor(name, shape, dt))

        def pb(name, shape):
            return ctx.enter_context(nc.psum_tensor(name, shape, F32))

        def sem(name):
            return ctx.enter_context(nc.semaphore(name))

        WP = sb("WP", [C, C])
        BP = sb("BP", [P, C])
        WG = sb("WG", [C, EXPERTS])
        BG = sb("BG", [1, EXPERTS])
        ident = sb("ident2", [P, P])
        ones = sb("ones", [1, P])
        NUM = sb("NUM", [C, N])
        DEN = sb("DEN", [C, N])
        HB = sb("HB", [P, NT, C])
        H1 = sb("H1", [P, NT, C])
        HO = sb("HO", [P, NT, C])
        STATS = sb("STATS2", [P, NT, 6])
        MV = sb("MV2", [P, NT, 2])
        STD = sb("STD2", [P, NT])
        RSTD = sb("RSTD2", [P, NT])
        XN = sb("XN2", [P, NT, C])
        XNT = sb("XNT2", [C, N])
        part_sum = sb("part_sum", [C, NG])
        mean = sb("mean", [C, 1])
        logits = sb("logits", [1, EXPERTS])
        top = sb("top", [1, 8])
        topi = sb("topi", [1, 8], U32)
        negm = sb("negm", [1, 1])
        ex = sb("ex", [1, EXPERTS])
        den = sb("den", [1, 1])
        gate = sb("gate", [1, 1])
        gcol = sb("gcol", [P, 1])
        gb = sb("gb", [P, C])
        WS = sb("WS", [C, C])
        BS = sb("BS", [1, C])

        pj_ps = pb("pj_ps", [P, 2, 512])
        tr_ps = pb("tr2_ps", [P, 2, 512])
        ff_ps = pb("ff_ps", [P, 2, 512])
        lg_ps = pb("lg_ps", [P, 512])
        bc_ps = pb("bc_ps", [P, 512])

        weights_in = sem("c_weights_in")
        num_in = sem("num_in")
        h_in = sem("h_in")
        rec_done = sem("rec_done")
        attn_ready = sem("attn_ready")
        hb_ready = sem("hb_ready")
        projected = sem("projected")
        h1_ready = sem("h1_ready")
        stats_done = sem("c_stats_done")
        std_done = sem("c_std_done")
        rstd_done = sem("c_rstd_done")
        xn_ready = sem("c_xn_ready")
        transposed = sem("c_transposed")
        xnt_ready = sem("c_xnt_ready")
        passed = sem("c_passed")
        route = sem("route")
        logits_done = sem("logits_done")
        ex_done = sem("ex_done")
        expert_in = sem("expert_in")
        bc_done = sem("bc_done")
        bc_copied = sem("bc_copied")
        ho_ready = sem("ho_ready")
        ffn_done = sem("ffn_done")
        out_ready = sem("out_ready")
        out_stored = sem("out_stored")
        ones_set = sem("ones_set")
        block = ctx.enter_context(nc.Block())
        RS = 8

        @block.sync
        def _(sp):
            for s in (h1_ready, xnt_ready, out_ready):
                sp.sem_inc(s, 1)
            sp.sem_inc(out_stored, 32)
            for dst, src in ((WP[:], io["w_proj"]), (BP[:], io["b_proj"].partition_broadcast(P)),
                             (WG[:], io["w_gate"]), (BG[:], io["b_gate"].partition_broadcast(1)),
                             (ident[:], io["ident"])):
                sp.dma_start(dst, src).then_inc(weights_in, 16)

            def load(b):
                for i, tile in enumerate((NUM, DEN)):
                    for u, (q0, _, _, pw) in enumerate(UNITS):
                        for j in range(4):
                            skip = 1024 * u - q0 if j == 0 else 0
                            q = q0 + j * pw + skip
                            sp.dma_start(tile[:, q:q + pw - skip],
                                         scr["o_img"][b, :, j, i, :, OFF[u] + skip:OFF[u] + pw])\
                                .then_inc(num_in, 16)

            load(0)
            sp.dma_start(HB[:], scr["h"][0]).then_inc(h_in, 16)

            def route_and_store(b):
                wait_apart(sp, route, RS * b + 5, passed)
                e = sp.value_load(topi[0:1, 0:1], min_val=0, max_val=EXPERTS - 1)
                sp.wait_ge(out_ready, NG * b + 1)
                sp.dma_start(WS[:], io["w_expert"][ds(e, 1)].rearrange("a d o -> (a d) o")).then_inc(expert_in, 16)
                sp.dma_start(BS[:], io["b_expert"][ds(e, 1)]).then_inc(expert_in, 16)
                sp.wait_ge(out_ready, NG * b + NG + 1)
                sp.dma_start(out[b, 0:P * (NT - 1), :].rearrange("(t p) c -> p t c", p=P),
                             HO[:, 0:NT - 1, :]).then_inc(out_stored, 16)
                sp.dma_start(out[b, P * (NT - 1):N, :], HO[0:LAST, NT - 1, :]).then_inc(out_stored, 16)

            with sp.Fori(0, B - 1) as b:
                sp.wait_ge(h1_ready, NG * b + NG + 1)
                load(b + 1)
                sp.dma_start(HB[:], scr["h"][b + 1]).then_inc(h_in, 16)
                route_and_store(b)
            route_and_store(B - 1)
            sp.wait_ge(out_stored, 32 * (B + 1))

        @block.gpsimd
        def _(pool):
            nc.gpsimd.memset(ones[:], 1.0).then_inc(ones_set, 1)
            pool.wait_ge(weights_in, 5 * 16)

            def whole(fn):
                fn(P, 0, NT - 1)
                return fn(LAST, NT - 1, NT)

            with pool.Fori(0, B) as b:
                pool.wait_ge(h_in, 16 * b + 16)
                whole(lambda r, a, z: nc.gpsimd.tensor_tensor(
                    HB[0:r, a:z, :], HB[0:r, a:z, :], BP[0:r, None, :].to_broadcast([r, z - a, C]) if z - a > 1
                    else BP[0:r, None, :], ALU.add)).then_inc(hb_ready, 1)
                pool.wait_ge(bc_copied, 2 * b + 2)
                pool.wait_ge(out_stored, 32 * b + 32)
                whole(lambda r, a, z: nc.gpsimd.tensor_tensor(
                    HO[0:r, a:z, :], H1[0:r, a:z, :], gb[0:r, None, :].to_broadcast([r, z - a, C]) if z - a > 1
                    else gb[0:r, None, :], ALU.add)).then_inc(ho_ready, 1)

        @block.scalar
        def _(act):
            with act.Fori(0, B) as b:
                act.wait_ge(stats_done, 3 * b + 3)
                nc.scalar.activation(STD[:], MV[:, :, 1], ACT.Sqrt).then_inc(std_done, 1)
                for g, n in GROUPS:
                    rows = LAST if g == NG - 1 else n * P
                    act.wait_ge(transposed, NG * b + g + 1)
                    if g == 0:
                        act.wait_ge(out_ready, NG * b + 1)
                    nc.scalar.activation(XNT[:, 4 * g * P:4 * g * P + rows], tr_ps[:, g % 2, 0:rows],
                                         ACT.Copy, accum_out=part_sum[:, g:g + 1]).then_inc(xnt_ready, 1)
                act.wait_ge(route, RS * b + 6)
                nc.scalar.activation(ex[:], logits[:], ACT.Exp, bias=negm[:], accum_out=den[:]).then_inc(ex_done, 1)

        @block.vector
        def _(dve):
            nc.vector.memset(MV[:], 1.0).then_inc(xn_ready, 1)
            dve.wait_ge(xn_ready, 1)
            dve.wait_ge(weights_in, 5 * 16)
            with dve.Fori(0, B) as b:
                dve.wait_ge(num_in, 24 * 16 * b + 24 * 16)
                nc.vector.reciprocal(DEN[:], DEN[:]).then_inc(rec_done, 1)
                dve.wait_ge(rec_done, b + 1)
                nc.vector.tensor_tensor(NUM[:], NUM[:], DEN[:], ALU.mult).then_inc(attn_ready, 1)
                dve.wait_ge(hb_ready, b + 1)
                for g, n in GROUPS:
                    rows = LAST if g == NG - 1 else P
                    dve.wait_ge(projected, NG * b + g + 1)
                    nc.vector.tensor_tensor(H1[0:rows, 4 * g:4 * g + n, :],
                                            pj_ps[0:rows, g % 2, 0:n * C].rearrange("p (t c) -> p t c", c=C),
                                            HB[0:rows, 4 * g:4 * g + n, :], ALU.add).then_inc(h1_ready, 1)
                    dve.wait_ge(h1_ready, NG * b + g + 2)
                    for t in range(4 * g, 4 * g + n):
                        rows = LAST if t == NT - 1 else P
                        last = nc.vector.bn_stats(STATS[0:rows, t, :], H1[0:rows, t, :])
                last.then_inc(stats_done, 1)
                wait_apart(dve, stats_done, 3 * b + 1, passed)
                for t in range(NT):
                    rows = LAST if t == NT - 1 else P
                    last = nc.vector.bn_aggr(MV[0:rows, t, :], STATS[0:rows, t, :])
                last.then_inc(stats_done, 1)
                dve.wait_ge(stats_done, 3 * b + 2)
                nc.vector.tensor_scalar(MV[:, :, 1], MV[:, :, 1], EPS, None, ALU.add).then_inc(stats_done, 1)
                dve.wait_ge(std_done, b + 1)
                nc.vector.reciprocal(RSTD[:], STD[:]).then_inc(rstd_done, 1)
                dve.wait_ge(rstd_done, b + 1)
                for g, n in GROUPS:
                    for t in range(4 * g, 4 * g + n):
                        rows = LAST if t == NT - 1 else P
                        last = nc.vector.tensor_scalar(XN[0:rows, t, :], H1[0:rows, t, :], MV[0:rows, t, 0:1],
                                                       RSTD[0:rows, t:t + 1], ALU.subtract, ALU.mult)
                    last.then_inc(xn_ready, 1)
                dve.wait_ge(xnt_ready, NG * b + NG + 1)
                nc.vector.tensor_reduce(mean[:], part_sum[:], AX.X, ALU.add).then_inc(route, 1)
                dve.wait_ge(route, RS * b + 1)
                nc.vector.tensor_scalar(mean[:], mean[:], 1.0 / N, None, ALU.mult).then_inc(route, 1)
                dve.wait_ge(logits_done, b + 1)
                nc.vector.tensor_tensor(logits[:], lg_ps[0:1, 0:EXPERTS], BG[:], ALU.add).then_inc(route, 1)
                wait_apart(dve, route, RS * b + 3, passed)
                nc.vector.max(top[:], logits[:]).then_inc(route, 1)
                wait_apart(dve, route, RS * b + 4, passed)
                nc.vector.max_index(topi[:], top[:], logits[:]).then_inc(route, 1)
                nc.vector.tensor_scalar(negm[:], top[:, 0:1], -1.0, None, ALU.mult).then_inc(route, 1)
                dve.wait_ge(ex_done, b + 1)
                nc.vector.reciprocal(den[:], den[:]).then_inc(route, 1)
                dve.wait_ge(route, RS * b + 7)
                nc.vector.tensor_scalar(gate[:], den[:], 1.0, None, ALU.mult).then_inc(route, 1)
                dve.wait_ge(bc_done, b + 1)
                nc.vector.tensor_copy(gcol[:], bc_ps[:, 0:1]).then_inc(bc_copied, 1)
                dve.wait_ge(bc_copied, 2 * b + 1)
                nc.vector.tensor_scalar(gb[:], bc_ps[:, 4:4 + C], gcol[:], None, ALU.mult).then_inc(bc_copied, 1)
                dve.wait_ge(ho_ready, b + 1)
                for g, n in GROUPS:
                    rows = LAST if g == NG - 1 else P
                    dve.wait_ge(ffn_done, NG * b + g + 1)
                    nc.vector.scalar_tensor_tensor(HO[0:rows, 4 * g:4 * g + n, :],
                                                   ff_ps[0:rows, g % 2, 0:n * C].rearrange("p (t c) -> p t c", c=C),
                                                   gcol[0:rows, :], HO[0:rows, 4 * g:4 * g + n, :],
                                                   ALU.mult, ALU.add).then_inc(out_ready, 1)

        @block.tensor
        def _(pe):
            pe.wait_ge(weights_in, 5 * 16)
            pe.wait_ge(ones_set, 1)
            with pe.Fori(0, B) as b:
                pe.wait_ge(attn_ready, b + 1)
                for g, n in GROUPS:
                    pe.wait_ge(h1_ready, NG * b + 1 + max(g - 1, 0))
                    for t in range(4 * g, 4 * g + n):
                        rows = LAST if t == NT - 1 else P
                        last = nc.tensor.matmul(pj_ps[0:rows, g % 2, (t % 4) * C:(t % 4 + 1) * C],
                                                NUM[:, t * P:t * P + rows], WP[:], start=True, stop=True)
                    last.then_inc(projected, 1)
                for g, n in GROUPS:
                    pe.wait_ge(xn_ready, NG * b + g + 2)
                    pe.wait_ge(xnt_ready, NG * b + 1 + max(g - 1, 0))
                    for t in range(4 * g, 4 * g + n):
                        rows = LAST if t == NT - 1 else P
                        last = nc.tensor.transpose(tr_ps[:, g % 2, (t % 4) * P:(t % 4) * P + rows],
                                                   XN[0:rows, t, :], ident[0:rows, 0:rows])
                    last.then_inc(transposed, 1)
                pe.wait_ge(route, RS * b + 2)
                nc.tensor.matmul(lg_ps[0:1, 0:EXPERTS], mean[:], WG[:], start=True, stop=True).then_inc(logits_done, 1)
                pe.wait_ge(route, RS * b + 8)
                pe.wait_ge(expert_in, 32 * b + 32)
                nc.tensor.matmul(bc_ps[:, 0:1], ones[:], gate[:], start=True, stop=True)
                nc.tensor.matmul(bc_ps[:, 4:4 + C], ones[:], BS[:], start=True, stop=True).then_inc(bc_done, 1)
                for g, n in GROUPS:
                    pe.wait_ge(out_ready, NG * b + 1 + max(g - 1, 0))
                    for t in range(4 * g, 4 * g + n):
                        rows = LAST if t == NT - 1 else P
                        last = nc.tensor.matmul(ff_ps[0:rows, g % 2, (t % 4) * C:(t % 4 + 1) * C],
                                                XNT[:, t * P:t * P + rows], WS[:], start=True, stop=True)
                    last.then_inc(ffn_done, 1)


def vit_tower(nc, io, out):
    def dram(name, shape, dt=F32):
        return nc.dram_tensor(name, shape, dt, kind="Internal").ap()

    qk = dram("qk_scratch", (B, 2, 3, C, N), BF16)
    h = dram("h_scratch", (B, P, NT, C))
    v = dram("v_scratch", (B, P, HEADS, NT, HD))
    o = dram("o_scratch", (GH, P, OW))
    shift = dram("shift_scratch", (GH, SHIFT_ROWS, NSH), BF16)

    def qk_by_head(g, side, part):
        flat = qk.rearrange("b s q r n -> b (s q) r n")
        img, head = g // HEADS, g % HEADS
        return flat[ds(img, 1), 3 * side + part, ds(head * HD, HD), :].rearrange("a r n -> (a r) n")

    def v_by_head(g):
        return v[ds(g // HEADS, 1), :, ds(g % HEADS, 1), :, :].rearrange("a p b t d -> (a p) (b t) d")

    scr = {
        "qk": qk, "h": h, "v": v, "o": o, "shift": shift,
        "qk_head": qk_by_head, "v_head": v_by_head,
        "o_img": o.rearrange("(b h) (j i d) w -> b h j i d w", b=B, j=4, i=2),
    }
    with nc.sbuf_tensor("flag", [1, 1], U32) as flag:
        phase_embed_qkv(nc, io, scr, flag)
        phase_maxima(nc, scr, flag)
        phase_attention(nc, scr)
        phase_project_ffn(nc, io, scr, out)


def kernel(x, cls_tok, L0_tok_W, L0_tok_b, L0_tok_cls, L0_attn_Wqkv, L0_attn_bqkv, L0_attn_Wproj, L0_attn_bproj,
           L0_ffn_Wg, L0_ffn_bg, L0_ffn_We, L0_ffn_be):
    import numpy as np
    import concourse.bacc as bacc
    from concourse import mybir as _mybir
    from concourse.bass_utils import run_bass_kernel_spmd

    x, cls_tok, W, b, cls = (np.asarray(a) for a in (x, cls_tok, L0_tok_W, L0_tok_b, L0_tok_cls))
    Wqkv, bqkv, Wproj = (np.asarray(a) for a in (L0_attn_Wqkv, L0_attn_bqkv, L0_attn_Wproj))

    freqs = (1.0 / np.float32(THETA) ** (np.arange(0, HD, 2, dtype=np.float32) / np.float32(HD))).astype(np.float32)
    angles = np.outer(np.arange(N, dtype=np.float32), freqs).astype(np.float32)
    comp = np.arange(C) % HD
    sign = np.where(comp % 2 == 0, -1.0, 1.0).astype(np.float32)[:, None]
    cos = np.ascontiguousarray(np.cos(angles).T[comp // 2])
    sin = np.ascontiguousarray(np.sin(angles).T[comp // 2]) * sign
    indicators = np.zeros((3, N), np.float32)
    indicators[0, 2:] = 1.0
    indicators[1, 0] = 1.0
    indicators[2, 1] = 1.0
    head_sum = np.zeros((C, HEADS), np.float32)
    head_sum[np.arange(C), np.arange(C) // HD] = 1.0

    def swapped(a):
        return a.reshape(C // 2, 2, -1)[:, ::-1].reshape(C, -1)

    Wq, Wk, Wv = Wqkv[0:C], Wqkv[C:2 * C], Wqkv[2 * C:]
    bq, bk, bv = bqkv[0:C, None], bqkv[C:2 * C, None], bqkv[2 * C:]
    arrays = {
        "patches": x.reshape(B, 3, GRID, PATCH, GRID, PATCH).transpose(0, 1, 3, 5, 2, 4).reshape(B, FEAT, NP_),
        "indicators": indicators,
        "w_embed": np.concatenate([b[None], cls_tok[0], cls[0], W.T]),
        "w_qk": np.stack([Wq.T, swapped(Wq).T, Wk.T, swapped(Wk).T], 1),
        "b_qk": np.concatenate([bq, swapped(bq), bk, swapped(bk)], 1),
        "w_v": Wv.T, "b_v": bv,
        "w_row": np.stack([Wq, Wk], 1),
        "head_sum": head_sum, "cos": cos, "sin": sin, "ident": np.eye(P, dtype=np.float32),
        "w_proj": Wproj.T, "b_proj": np.asarray(L0_attn_bproj),
        "w_gate": np.asarray(L0_ffn_Wg), "b_gate": np.asarray(L0_ffn_bg),
        "w_expert": np.asarray(L0_ffn_We), "b_expert": np.asarray(L0_ffn_be),
    }
    nc = bacc.Bacc("TRN2", target_bir_lowering=False, num_devices=1)
    io, feed = {}, {}
    for name, a in arrays.items():
        feed[f"in_{name}"] = np.ascontiguousarray(a)
        io[name] = nc.dram_tensor(f"in_{name}", a.shape, _mybir.dt.from_np(a.dtype), kind="ExternalInput").ap()
    out = nc.dram_tensor("out_0", (B, N, C), _mybir.dt.float32, kind="ExternalOutput").ap()
    vit_tower(nc, io, out)
    r = run_bass_kernel_spmd(nc, [feed], core_ids=[0])
    return r.results[0]["out_0"]
```

```python
from contextlib import ExitStack

import concourse.bass as bass
from concourse import mybir

F32 = mybir.dt.float32
BF16 = mybir.dt.bfloat16
U32 = mybir.dt.uint32
ALU = mybir.AluOpType
ACT = mybir.ActivationFunctionType
AX = mybir.AxisListType
ds = bass.ds

B = 8
IMG, PATCH = 224, 4
GRID = IMG // PATCH
NP_ = GRID * GRID
N = NP_ + 2
C = 128
FEAT = 3 * PATCH * PATCH
HEADS, HD = 8, 16
GH = B * HEADS
EXPERTS = 16
P = 128
NT = -(-N // P)
LAST = N - P * (NT - 1)
GROUPS = [(g, min(4, NT - 4 * g)) for g in range(-(-NT // 4))]
NG = len(GROUPS)
EPS = 1e-5
SCALE = HD ** -0.5
THETA = 10000.0

CW = 448
NC = N // CW
CHUNKS = [(c * CW, CW if c < NC - 1 else N - CW * (NC - 1)) for c in range(NC)]
CMAX = CHUNKS[-1][1]

UNITS = [(0, 512, 2, 256), (1024, 512, 2, 256), (N - 1092, 364, 3, 273)]
NU = len(UNITS)
UMAX = 1092
OFF = [0, 256, 512]
OW = 512 + 273
OLOADS = 4 * NU
UPH = NU * NT
UPI = UPH * HEADS

A_KINDS = ["embed", "turn", "value", "query", "key"]
A_PIECES = [(kind, i) for kind in A_KINDS for i in range(NG)]
NA = len(A_PIECES)
C_PIECES = ([("project", i) for i in range(NG)] + [("turn", i) for i in range(NG)] +
            [("route", 0), ("gate", 0)] + [("expert", i) for i in range(NG)])
NCP = len(C_PIECES)
A_AT = {h: dict(zip((2, 5, 8, 11, 14, 17, 20), range(NG * h, NG * h + NG))) for h in range(5)}
C_AT = {5: dict(zip((10, 12, 14, 16, 18, 20, 22), range(0, NG))),
        6: dict(zip((2, 5, 8, 11, 14, 17, 20, 22), range(NG, 2 * NG + 1))),
        7: dict(zip((3, 7, 9, 12, 14, 17, 20, 22), range(2 * NG + 1, NCP)))}
MAXIMA_AT = (5, 1)
NMAX = 7
WMAX = 449
MAX_AT = [min(c * (WMAX - 1), N - WMAX) for c in range(NMAX)]
AGG_STEPS = 16
C_STEPS = AGG_STEPS + 2 + 1 + NG + 2 + 2
MPI = HEADS * NT * NMAX

Q_ROWS = [0, 1, 2, 0, 1, 0]
K_ROWS = [0, 0, 0, 1, 1, 2]
PAIRS = len(Q_ROWS)
KR = PAIRS * HD
SHIFT_ROWS = 2
KS = KR + SHIFT_ROWS
NSH = NT * P
LOADS = 2 * PAIRS + 1

SAFE = 60.0


def wait_apart(engine, sem, count, passed):
    engine.wait_ge(sem, count)
    engine.sem_inc(passed, 1)


def rows_of(t):
    return LAST if t == NT - 1 else P


def vit_tower(nc, io, out):
    def dram(name, shape, dt=F32):
        return nc.dram_tensor(name, shape, dt, kind="Internal").ap()

    qk_s = dram("qk_scratch", (B, 2, 3, C, N), BF16)
    h_s = dram("h_scratch", (B, P, NT, C))
    v_s = dram("v_scratch", (B, P, HEADS, NT, HD))
    o_s = dram("o_scratch", (GH, P, OW))
    shift_s = dram("shift_scratch", (GH, SHIFT_ROWS, NSH), BF16)
    o_img = o_s.rearrange("(b h) (j i d) w -> b h j i d w", b=B, j=4, i=2)

    def following(b, k=1):
        return nc.s_assert_within(b + k, k, B - 1, skip_runtime_bounds_check_because="the If around it sees to it")

    def previous(b):
        return nc.s_assert_within(b - 1, 0, B - 2, skip_runtime_bounds_check_because="the If around it sees to it")

    ctx = ExitStack()
    with ctx:
        def sb(name, shape, dt=F32):
            return ctx.enter_context(nc.sbuf_tensor(name, shape, dt))

        def sem(name):
            return ctx.enter_context(nc.semaphore(name))

        WE = sb("WE", [3 + FEAT, C])
        WQK = sb("WQK", [C, 2, C])
        BQK = sb("BQK", [C, 2])
        WV = sb("WV", [C, C])
        BV = sb("BV", [P, C])
        COS = sb("COS", [C, N])
        SIN = sb("SIN", [C, N])
        ident = sb("ident", [P, P])
        WP = sb("WP", [C, C])
        BP = sb("BP", [P, C])
        WG = sb("WG", [C, EXPERTS])
        BG = sb("BG", [1, EXPERTS])
        ones = sb("ones", [1, P])
        WROW = sb("WROW", [C, 2, C])
        HSUM = sb("HSUM", [C, HEADS])
        sq = sb("sq", [C, C])
        ss = sb("ss", [C, 2])
        nrm = sb("nrm", [C, 2])
        ab = sb("ab", [C, 2])
        bound = sb("bound", [C, 4])
        hq = sb("hq", [1, 3 * HEADS])
        flag = sb("flag", [1, 1], U32)
        DX = sb("DX", [C, N])
        XS, DEN = DX[0:3 + FEAT, :], DX
        H = sb("H", [P, NT, C])
        XN = sb("XN", [P, NT, C])
        XNT = sb("XNT", [C, N])
        VRES = sb("VRES", [P, NT * C])
        V = VRES[:, :].rearrange("p (h t d) -> p h t d", h=HEADS, d=HD)
        H1 = VRES[:, :].rearrange("p (t c) -> p t c", c=C)
        KQM = VRES[:, :].bitcast(BF16)
        KM, QM = KQM[0:KR, 0:N], KQM[0:KR, N:2 * N]
        PARTS = sb("PARTS", [C, 2 * 3 * N], BF16)
        NUM = PARTS[:, 0:2 * N].bitcast(F32)

        def part(side, p, s, w):
            at = (3 * side + p) * N + s
            return PARTS[:, at:at + w]

        STATS = sb("STATS", [P, NT, 6])
        MV = sb("MV", [P, NT, 2])
        RSTD = sb("RSTD", [P, NT])
        NEWT = sb("NEWT", [P, NT])
        QB = sb("QB", [C, CMAX])
        QSH = sb("QSH", [C, CMAX])
        QF = sb("QF", [C, CMAX])
        RF = sb("RF", [C, CMAX])
        MXC = sb("MXC", [P, NMAX])
        MX = sb("MX", [P, NT])
        NM = sb("NM", [P, NT])
        NHL = sb("NHL", [P, SHIFT_ROWS, NT], BF16)
        part_sum = sb("part_sum", [C, NG])
        mean = sb("mean", [C, 1])
        logits = sb("logits", [1, EXPERTS])
        top = sb("top", [1, 8])
        topi = sb("topi", [1, 8], U32)
        negm = sb("negm", [1, 1])
        ex = sb("ex", [1, EXPERTS])
        den = sb("den", [1, 1])
        gate = sb("gate", [1, 1])
        gcol = sb("gcol", [P, 1])
        gb = sb("gb", [P, C])
        WS = sb("WS", [C, C])
        BS = sb("BS", [1, C])
        KA = [sb(f"KA{i}", [KS, N], BF16) for i in range(2)]
        QA = [sb(f"QA{i}", [KS, N], BF16) for i in range(2)]
        VH = [sb(f"VH{i}", [P, NT, HD]) for i in range(2)]
        VST = [sb(f"VST{i}", [P, 2 * HD]) for i in range(2)]
        E = [sb(f"E{u}", [P, UMAX]) for u in range(NU)]
        OB = [sb(f"OB{i}", [P, OW]) for i in range(2)]
        S = [ctx.enter_context(nc.psum_tensor(f"S{i}", [P, 3, 512], F32)) for i in range(2)]
        PO = [ctx.enter_context(nc.psum_tensor(f"PO{i}", [P, 512], F32)) for i in range(2)]

        early_in = sem("early_in")
        weights_in = sem("weights_in")
        consts = sem("consts")
        zeros_ready = sem("zeros_ready")
        shift_zeroed = sem("shift_zeroed")
        bound_step = sem("bound_step")
        exp_loaded = sem("exp_loaded")
        passed = sem("passed")
        pixels_in = sem("pixels_in")
        a_issued = sem("a_issued")
        a_drained = sem("a_drained")
        a_chain = sem("a_chain")
        xn_ready = sem("xn_ready")
        parts_ready = sem("parts_ready")
        h_stored = sem("h_stored")
        v_stored = sem("v_stored")
        qk_stored = sem("qk_stored")
        m_loaded = sem("m_loaded")
        m_scored = sem("m_scored")
        m_reduced = sem("m_reduced")
        m_chain = sem("m_chain")
        m_split = sem("m_split")
        m_stored = sem("m_stored")
        qk_in = [sem(f"qk_in{i}") for i in range(2)]
        v_in = [sem(f"v_in{i}") for i in range(2)]
        scores = sem("scores")
        probs = sem("probs")
        used = sem("used")
        v_staged = sem("v_staged")
        o_out = [sem(f"o_out{i}") for i in range(2)]
        o_stored = [sem(f"o_stored{i}") for i in range(2)]
        den_in = sem("den_in")
        num_in = sem("num_in")
        h_in = sem("h_in")
        c_issued = sem("c_issued")
        c_drained = sem("c_drained")
        c_chain = sem("c_chain")
        attn_ready = sem("attn_ready")
        xn2_ready = sem("xn2_ready")
        routed = sem("routed")
        ex_done = sem("ex_done")
        expert_in = sem("expert_in")
        out_stored = sem("out_stored")
        block = ctx.enter_context(nc.Block())

        @block.sync
        def _(sp):
            for s, v in ((scores, 1), (used, 4), (v_staged, 1), (o_out[0], 1), (o_out[1], 1), (o_stored[0], 16),
                         (o_stored[1], 16), (attn_ready, 1), (out_stored, 64), (m_reduced, 1), (m_stored, 32),
                         (den_in, OLOADS * 16), (num_in, OLOADS * 16), (h_in, 16), (c_issued, NCP),
                         (c_drained, NCP), (c_chain, C_STEPS),
                         (xn2_ready, NG), (routed, 4), (ex_done, 1), (expert_in, 32)):
                sp.sem_inc(s, v)

            def load_pixels(a):
                sp.dma_start(XS[0:3, :], io["indicators"]).then_inc(pixels_in, 16)
                sp.dma_start(XS[3:3 + FEAT, :], io["pixels"][a]).then_inc(pixels_in, 16)

            load_pixels(0)
            for dst, src, arrived in ((WE[:], io["w_embed"], early_in), (WROW[:], io["w_row"], early_in),
                             (BQK[:], io["b_qk"], early_in), (HSUM[:], io["head_sum"], early_in),
                             (ident[:], io["ident"], early_in), (WV[:], io["w_v"], early_in),
                             (BV[:], io["b_v"].partition_broadcast(P), early_in), (WQK[:], io["w_qk"], early_in),
                             (COS[:], io["cos"], weights_in), (SIN[:], io["sin"], weights_in),
                             (WP[:], io["w_proj"], weights_in),
                             (BP[:], io["b_proj"].partition_broadcast(P), weights_in),
                             (WG[:], io["w_gate"], weights_in),
                             (BG[:], io["b_gate"].partition_broadcast(1), weights_in)):
                sp.dma_start(dst, src).then_inc(arrived, 16)
            sp.wait_ge(zeros_ready, 1)
            sp.dma_start(shift_s.rearrange("g r n -> (g r n)").rearrange("(p f) -> p f", p=P),
                         KQM[:, 0:GH * SHIFT_ROWS * NSH // P]).then_inc(shift_zeroed, 16)
            sp.wait_ge(bound_step, 10)
            needed = sp.value_load(flag[0:1, 0:1], min_val=0, max_val=1)

            def store_h(a):
                sp.wait_ge(a_drained, NA * a + NG)
                sp.dma_start(h_s[a], H[:]).then_inc(h_stored, 16)

            def store_v(a):
                sp.wait_ge(a_drained, NA * a + 3 * NG)
                sp.dma_start(v_s[a], V).then_inc(v_stored, 16)

            def store_parts(a, side):
                sp.wait_ge(parts_ready, 2 * a + side + 1)
                for p in range(3):
                    sp.dma_start(qk_s[a, side, p], part(side, p, 0, N)).then_inc(qk_stored, 16)

            def rows(a, head, side, p):
                return qk_s[a, side, p, ds(head * HD, HD), :]

            def find_maxima(a):
                sp.wait_ge(qk_stored, 96 * a + 96)
                sp.wait_ge(v_stored, 16 * a + 16)
                wait_apart(sp, shift_zeroed, 16, passed)
                with sp.Fori(0, HEADS) as head:
                    sp.wait_ge(m_reduced, MPI * a + NT * NMAX * head + 1)
                    for i in range(PAIRS):
                        sp.dma_start(QM[i * HD:(i + 1) * HD, :], rows(a, head, 0, Q_ROWS[i])).then_inc(m_loaded, 16)
                        sp.dma_start(KM[i * HD:(i + 1) * HD, :], rows(a, head, 1, K_ROWS[i])).then_inc(m_loaded, 16)
                    sp.wait_ge(m_split, HEADS * a + head + 1)
                    with nc.allow_non_contiguous_dma(reason="a column of maxima becomes a row"):
                        for r in range(SHIFT_ROWS):
                            sp.dma_start(shift_s[ds(HEADS * a + head, 1), r, :].rearrange("g (t p) -> p (g t)", p=P),
                                         NHL[:, r, :]).then_inc(m_stored, 16)
                wait_apart(sp, m_stored, 32 * HEADS * a + 32 * HEADS + 32, passed)

            def load_head(a, head, par):
                for i in range(PAIRS):
                    sp.dma_start(QA[par][i * HD:(i + 1) * HD, :],
                                 qk_s[a, 0, Q_ROWS[i], head * HD:(head + 1) * HD, :]).then_inc(qk_in[par], 16)
                    sp.dma_start(KA[par][i * HD:(i + 1) * HD, :],
                                 qk_s[a, 1, K_ROWS[i], head * HD:(head + 1) * HD, :]).then_inc(qk_in[par], 16)
                sp.dma_start(QA[par][KR:KS, :], shift_s[HEADS * a + head, :, 0:N]).then_inc(qk_in[par], 16)
                sp.dma_start(VH[par][:], v_s[a, :, head, :, :]).then_inc(v_in[par], 16)

            def store_o(g, par):
                sp.wait_ge(o_out[0], g + 2)
                sp.wait_ge(o_out[1], g + 2)
                sp.dma_start(o_s[g], OB[par][:]).then_inc(o_stored[par], 16)

            def load_attention(c, turn):
                for par in range(2):
                    sp.wait_ge(o_stored[par], 16 * (HEADS // 2) * turn + 16)
                for i, tile, arrived in ((1, DEN, den_in), (0, NUM, num_in)):
                    for u, (q0, _, _, pw) in enumerate(UNITS):
                        for j in range(4):
                            skip = 1024 * u - q0 if j == 0 else 0
                            q = q0 + j * pw + skip
                            sp.dma_start(tile[:, q:q + pw - skip],
                                         o_img[c, :, j, i, :, OFF[u] + skip:OFF[u] + pw]).then_inc(arrived, 16)
                sp.dma_start(H[:], h_s[c]).then_inc(h_in, 16)

            def load_expert(turn):
                wait_apart(sp, routed, 4 * turn + 2, passed)
                e = sp.value_load(topi[0:1, 0:1], min_val=0, max_val=EXPERTS - 1)
                sp.dma_start(WS[:], io["w_expert"][ds(e, 1)].rearrange("a d o -> (a d) o")).then_inc(expert_in, 16)
                sp.dma_start(BS[:], io["b_expert"][ds(e, 1)]).then_inc(expert_in, 16)

            def store_out(c, turn):
                sp.wait_ge(c_drained, NCP * turn + NCP)
                sp.dma_start(out[c, 0:P * (NT - 1), :].rearrange("(t p) c -> p t c", p=P),
                             H1[:, 0:NT - 1, :]).then_inc(out_stored, 16)
                sp.dma_start(out[c, P * (NT - 1):N, :], H1[0:LAST, NT - 1, :]).then_inc(out_stored, 16)

            store_h(0)
            load_pixels(1)
            store_v(0)
            store_parts(0, 0)
            store_parts(0, 1)
            with sp.If(needed > 0):
                find_maxima(0)
            sp.wait_ge(qk_stored, 96)
            sp.wait_ge(v_stored, 16)
            sp.wait_ge(shift_zeroed, 16)
            load_head(0, 0, 0)
            with sp.Fori(0, B) as b:
                for h in range(HEADS):
                    g = HEADS * b + h
                    if h < HEADS - 1:
                        sp.wait_ge(scores, UPH * g + 1)
                        sp.wait_ge(v_staged, NT * g + 1)
                        load_head(b, h + 1, (h + 1) % 2)
                    else:
                        with sp.If(b < B - 1):
                            sp.wait_ge(scores, UPH * g + 1)
                            sp.wait_ge(v_staged, NT * g + 1)
                            sp.wait_ge(qk_stored, 96 * b + 192)
                            sp.wait_ge(v_stored, 16 * b + 32)
                            load_head(following(b), 0, 0)
                    if h in (0, 2, 3, 4):
                        with sp.If(b < B - 1):
                            if h == 0:
                                store_h(following(b))
                            elif h == 2:
                                store_v(following(b))
                            elif h == 3:
                                store_parts(following(b), 0)
                            else:
                                sp.wait_ge(h_stored, 16 * b + 32)
                                sp.wait_ge(xn_ready, NG * b + 2 * NG)
                                wait_apart(sp, qk_stored, 96 * b + 144, passed)
                    if h == 4:
                        with sp.If(b > 0):
                            load_attention(previous(b), b)
                        with sp.If(b < B - 1):
                            store_parts(following(b), 1)
                    if h == 5:
                        with sp.If(b + (1 - needed) * B < B - 1):
                            find_maxima(following(b))
                    if h == 6:
                        with sp.If(b < B - 2):
                            sp.wait_ge(attn_ready, b + 1)
                            load_pixels(following(b, 2))
                        with sp.If(b > 0):
                            load_expert(b)
                    if h == 7:
                        with sp.If(b > 0):
                            store_out(previous(b), b)
                    store_o(g, h % 2)
            load_attention(B - 1, B)
            load_expert(B)
            store_out(B - 1, B)
            sp.wait_ge(out_stored, 32 * B + 64)

        @block.gpsimd
        def _(pool):
            nc.gpsimd.memset(VRES[:], 0.0).then_inc(zeros_ready, 1)
            nc.gpsimd.memset(ones[:], 1.0).then_inc(consts, 1)
            for i in range(2):
                nc.gpsimd.memset(VST[i][:, HD:], 1.0).then_inc(consts, 1)

            def stage(gk, par, kt, slot):
                wait_apart(pool, used, NU * gk + 1, passed)
                nc.gpsimd.tensor_copy(VST[slot][:, 0:HD], VH[par][:, kt, :] if isinstance(kt, int) else
                                      VH[par][:, ds(kt, 1), :].rearrange("p a d -> p (a d)")).then_inc(v_staged, 1)

            with pool.Fori(0, GH // 2) as pair:
                for par in range(2):
                    g = 2 * pair + par
                    wait_apart(pool, v_in[par], 16 * pair + 16, passed)
                    with pool.Fori(0, NT // 2) as half:
                        for k in range(2):
                            stage(NT * g + 2 * half + k, par, 2 * half + k, (par + k) % 2)
                    stage(NT * g + NT - 1, par, NT - 1, (par + NT - 1) % 2)

        @block.scalar
        def _(act):
            act.wait_ge(early_in, 8 * 16)
            nc.scalar.activation(sq[:], WROW[:, 0, :], ACT.Square, accum_out=ss[:, 0:1]).then_inc(bound_step, 1)
            act.wait_ge(bound_step, 1)
            nc.scalar.activation(sq[:], WROW[:, 1, :], ACT.Square, accum_out=ss[:, 1:2]).then_inc(bound_step, 1)
            nc.scalar.activation(ab[:], BQK[:], ACT.Abs).then_inc(bound_step, 1)
            act.wait_ge(bound_step, 3)
            nc.scalar.activation(nrm[:], ss[:], ACT.Sqrt, scale=float(C)).then_inc(bound_step, 1)
            act.wait_ge(consts, 6)
            nc.scalar.activation(den[:], ones[0:1, 0:1], ACT.Exp).then_inc(exp_loaded, 1)

            def exp_tile(g, par, kt, ktp, rows):
                for u, (_, w, n, _) in enumerate(UNITS):
                    unit = UPH * g + NU * kt + u
                    act.wait_ge(scores, unit + 2)
                    act.wait_ge(used, unit + 2)
                    nc.scalar.activation(E[u][0:rows, 0:n * w].rearrange("p (n w) -> p n w", w=w),
                                         S[(par + ktp + u) % 2][0:rows, 0:n, 0:w], ACT.Exp,
                                         scale=SCALE).then_inc(probs, 1)

            def exp_head(g, par):
                with act.Fori(0, NT // 2) as half:
                    for k in range(2):
                        exp_tile(g, par, 2 * half + k, k, P)
                exp_tile(g, par, NT - 1, 0, LAST)

            def exp_logits(turn):
                act.wait_ge(routed, 4 * turn + 3)
                nc.scalar.activation(ex[:], logits[:], ACT.Exp, bias=negm[:], accum_out=den[:]).then_inc(ex_done, 1)

            with act.Fori(0, B) as b:
                with act.Fori(0, HEADS // 2 - 1) as pair:
                    for par in range(2):
                        exp_head(HEADS * b + 2 * pair + par, par)
                exp_head(HEADS * b + HEADS - 2, 0)
                with act.If(b > 0):
                    exp_logits(b)
                exp_head(HEADS * b + HEADS - 1, 1)
            exp_logits(B)

        @block.vector
        def _(dve):
            class Chain:
                def __init__(self, sem):
                    self.sem, self.per_image, self.k = sem, 0, 0

                def begin(self):
                    self.per_image, self.k = max(self.per_image, self.k), 0

                def link(self, ins, image, apart=False):
                    self.k += 1
                    ins.then_inc(self.sem, 1)
                    count = self.per_image * image + self.k
                    if apart and not isinstance(count, int):
                        wait_apart(dve, self.sem, count, passed)
                    else:
                        dve.wait_ge(self.sem, count)

            def groups(ps, n):
                return ps[:, 0:n * C].rearrange("p (t c) -> p t c", c=C)

            def statistics(src, g, n):
                for t in range(4 * g, 4 * g + n):
                    r = rows_of(t)
                    last = nc.vector.bn_stats(STATS[0:r, t, :], src[0:r, t, :])
                return last

            def aggregate(chain, image):
                for t in range(NT):
                    r = rows_of(t)
                    last = nc.vector.bn_aggr(MV[0:r, t, :], STATS[0:r, t, :])
                chain.link(last, image)
                v, y, z = MV[:, :, 1], RSTD[:], NEWT[:]
                chain.link(nc.vector.tensor_scalar(v, v, EPS, None, ALU.add), image)
                chain.link(nc.vector.tensor_scalar(NEWT[:].bitcast(U32), v.bitcast(U32), 1, None,
                                                   ALU.logical_shift_right), image)
                chain.link(nc.vector.tensor_scalar(RSTD[:].bitcast(U32), NEWT[:].bitcast(U32), -1.0,
                                                   float(0x5f3759df), ALU.mult, ALU.add), image)
                for _ in range(4):
                    chain.link(nc.vector.scalar_tensor_tensor(z, y, -0.5, y, ALU.mult, ALU.mult), image)
                    chain.link(nc.vector.tensor_tensor(z, z, v, ALU.mult), image)
                    chain.link(nc.vector.scalar_tensor_tensor(y, z, 1.5, y, ALU.add, ALU.mult), image)

            def normalise(src, g, ready):
                for t in range(4 * g, 4 * g + GROUPS[g][1]):
                    r = rows_of(t)
                    last = nc.vector.tensor_scalar(XN[0:r, t, :], src[0:r, t, :], MV[0:r, t, 0:1],
                                                   RSTD[0:r, t:t + 1], ALU.subtract, ALU.mult)
                last.then_inc(ready, 1)

            ac, cc, mc = Chain(a_chain), Chain(c_chain), Chain(m_chain)
            swap = [i ^ 1 for i in range(32)]

            def before_job(a, i, bank):
                kind, g = A_PIECES[i]
                later = not isinstance(a, int)
                if kind == "embed":
                    n = GROUPS[g][1]
                    r = LAST if g == NG - 1 else P
                    if g == 0 and later:
                        dve.wait_ge(h_stored, 16 * a)
                    dve.wait_ge(a_issued, NA * a + i + 1)
                    nc.vector.tensor_copy(H[0:r, 4 * g:4 * g + n, :], groups(bank, n)[0:r]).then_inc(a_drained, 1)
                    dve.wait_ge(a_drained, NA * a + i + 1)
                    last = statistics(H, g, n)
                    if g == NG - 1:
                        ac.link(last, a, apart=True)
                        aggregate(ac, a)
                        normalise(H, 0, xn_ready)
                elif kind == "turn":
                    w = LAST if g == NG - 1 else GROUPS[g][1] * P
                    dve.wait_ge(a_issued, NA * a + i + 1)
                    nc.vector.tensor_copy(XNT[:, 4 * g * P:4 * g * P + w], bank[:, 0:w]).then_inc(a_drained, 1)
                    if g < NG - 1:
                        normalise(H, g + 1, xn_ready)
                elif kind == "value":
                    n = GROUPS[g][1]
                    r = LAST if g == NG - 1 else P
                    if g == 0 and not later:
                        dve.wait_ge(shift_zeroed, 16)
                    if g == 0 and later:
                        dve.wait_ge(out_stored, 32 * a)
                        dve.wait_ge(v_stored, 16 * a)
                    dve.wait_ge(a_issued, NA * a + i + 1)
                    bias = BV[0:r, :].rearrange("p (h d) -> p h d", d=HD)[:, None]
                    nc.vector.tensor_tensor(V[0:r, :, 4 * g:4 * g + n, :].rearrange("p h t d -> p t h d"),
                                            bank[0:r, 0:n * C].rearrange("p (t h d) -> p t h d", h=HEADS, d=HD),
                                            bias.to_broadcast([r, n, HEADS, HD]) if n > 1 else bias,
                                            ALU.add).then_inc(a_drained, 1)
                else:
                    side = A_KINDS.index(kind) - 3
                    s, w = CHUNKS[g]
                    if kind == "query" and g == 0 and not later:
                        dve.wait_ge(weights_in, 6 * 16)
                    if g == 0 and later:
                        dve.wait_ge(qk_stored, 96 * a)
                    dve.wait_ge(a_issued, NA * a + i + 1)
                    nc.vector.tensor_scalar(QB[:, 0:w], bank[:, 0:w], BQK[:, side:side + 1], None,
                                            ALU.add).then_inc(a_drained, 1)
                    if later:
                        wait_apart(dve, a_drained, NA * a + i + 1, passed)
                    else:
                        dve.wait_ge(a_drained, NA * a + i + 1)
                    nc.vector.stream_shuffle(QSH[:, 0:w], QB[:, 0:w], swap)
                    ac.link(nc.vector.tensor_tensor(QF[:, 0:w], QB[:, 0:w], COS[:, s:s + w], ALU.mult), a)
                    ac.link(nc.vector.tensor_tensor(QSH[:, 0:w], QSH[:, 0:w], SIN[:, s:s + w], ALU.mult), a)
                    ac.link(nc.vector.tensor_tensor(QF[:, 0:w], QF[:, 0:w], QSH[:, 0:w], ALU.add), a)
                    ac.link(nc.vector.tensor_copy(part(side, 0, s, w), QF[:, 0:w]), a)
                    ac.link(nc.vector.tensor_tensor(RF[:, 0:w], QF[:, 0:w], part(side, 0, s, w), ALU.subtract), a)
                    ac.link(nc.vector.tensor_copy(part(side, 1, s, w), RF[:, 0:w]), a)
                    last = nc.vector.tensor_tensor(part(side, 2, s, w), RF[:, 0:w], part(side, 1, s, w), ALU.subtract)
                    if g == NG - 1:
                        last.then_inc(parts_ready, 1)
                    else:
                        ac.link(last, a)

            def maxima_job(a):
                with dve.Fori(0, HEADS) as head:
                    n0 = MPI * a + NT * NMAX * head

                    def tile(t, r):
                        for c in range(NMAX):
                            dve.wait_ge(m_scored, n0 + NMAX * t + c + 1)
                            nc.vector.tensor_reduce(MXC[0:r, c:c + 1], S[1][0:r, 2, 0:WMAX], AX.X,
                                                    ALU.max).then_inc(m_reduced, 1)
                        dve.wait_ge(m_reduced, n0 + NMAX * t + NMAX + 1)
                        nc.vector.tensor_reduce(MX[0:r, NT - 1:NT] if isinstance(t, int) else MX[0:r, ds(t, 1)],
                                                MXC[0:r, :], AX.X, ALU.max).then_inc(m_chain, 1)
                        wait_apart(dve, m_chain, (NT + 2) * (HEADS * a + head) + t + 1, passed)

                    with dve.Fori(0, NT - 1) as t:
                        tile(t, P)
                    tile(NT - 1, LAST)
                    dve.wait_ge(m_stored, 32 * (HEADS * a + head) + 32)
                    nc.vector.tensor_scalar(NM[:], MX[:], -1.0, None, ALU.mult).then_inc(m_chain, 1)
                    dve.wait_ge(m_chain, (NT + 2) * (HEADS * a + head) + NT + 1)
                    nc.vector.tensor_copy(NHL[:, 0, :], NM[:]).then_inc(m_chain, 1)
                    dve.wait_ge(m_chain, (NT + 2) * (HEADS * a + head) + NT + 2)
                    nc.vector.tensor_tensor(NHL[:, 1, :], NM[:], NHL[:, 0, :], ALU.subtract).then_inc(m_split, 1)

            def attention_job(turn):
                dve.wait_ge(den_in, OLOADS * 16 * (turn + 1))
                cc.link(nc.vector.reciprocal(DEN[:], DEN[:]), turn)
                dve.wait_ge(num_in, OLOADS * 16 * (turn + 1))
                nc.vector.tensor_tensor(NUM[:], NUM[:], DEN[:], ALU.mult).then_inc(attn_ready, 1)
                dve.wait_ge(h_in, 16 * turn + 16)
                cc.link(nc.vector.tensor_tensor(H[:], H[:], BP[:, None, :].to_broadcast([P, NT, C]), ALU.add), turn, apart=True)

            def after_job(turn, i, bank):
                kind, g = C_PIECES[i]
                n = GROUPS[g][1]
                r = LAST if g == NG - 1 else P
                if kind == "gate":
                    dve.wait_ge(ex_done, turn + 1)
                    nc.vector.reciprocal(gate[:], den[:]).then_inc(routed, 1)
                if kind == "route":
                    cc.link(nc.vector.tensor_reduce(mean[:], part_sum[:], AX.X, ALU.add), turn)
                    nc.vector.tensor_scalar(mean[:], mean[:], 1.0 / N, None, ALU.mult).then_inc(routed, 1)
                dve.wait_ge(c_issued, NCP * turn + i + 1)
                if kind == "project":
                    nc.vector.tensor_tensor(H1[0:r, 4 * g:4 * g + n, :], groups(bank, n)[0:r],
                                            H[0:r, 4 * g:4 * g + n, :], ALU.add).then_inc(c_drained, 1)
                    dve.wait_ge(c_drained, NCP * turn + i + 1)
                    last = statistics(H1, g, n)
                    if g == NG - 1:
                        cc.link(last, turn, apart=True)
                        aggregate(cc, turn)
                        normalise(H1, 0, xn2_ready)
                elif kind == "turn":
                    w = LAST if g == NG - 1 else n * P
                    nc.vector.tensor_copy(XNT[:, 4 * g * P:4 * g * P + w], bank[:, 0:w]).then_inc(c_drained, 1)
                    if g < NG - 1:
                        normalise(H1, g + 1, xn2_ready)
                    dve.wait_ge(c_drained, NCP * turn + i + 1)
                    cc.link(nc.vector.tensor_reduce(part_sum[:, g:g + 1], XNT[:, 4 * g * P:4 * g * P + w],
                                                    AX.X, ALU.add), turn)
                elif kind == "route":
                    nc.vector.tensor_tensor(logits[:], bank[0:1, 0:EXPERTS], BG[:], ALU.add).then_inc(c_drained, 1)
                    wait_apart(dve, c_drained, NCP * turn + i + 1, passed)
                    cc.link(nc.vector.max(top[:], logits[:]), turn, apart=True)
                    nc.vector.max_index(topi[:], top[:], logits[:]).then_inc(routed, 1)
                    nc.vector.tensor_scalar(negm[:], top[:, 0:1], -1.0, None, ALU.mult).then_inc(routed, 1)
                elif kind == "gate":
                    cc.link(nc.vector.tensor_copy(gcol[:], bank[:, 0:1]), turn)
                    nc.vector.tensor_scalar(gb[:], bank[:, 4:4 + C], gcol[:], None, ALU.mult).then_inc(c_drained, 1)
                    dve.wait_ge(c_drained, NCP * turn + i + 1)
                    nc.vector.tensor_tensor(H1[:, 0:NT - 1, :], H1[:, 0:NT - 1, :],
                                            gb[:, None, :].to_broadcast([P, NT - 1, C]), ALU.add)
                    cc.link(nc.vector.tensor_tensor(H1[0:LAST, NT - 1, :], H1[0:LAST, NT - 1, :], gb[0:LAST, :],
                                                    ALU.add), turn)
                else:
                    nc.vector.scalar_tensor_tensor(H1[0:r, 4 * g:4 * g + n, :], groups(bank, n)[0:r], gcol[0:r, :],
                                                   H1[0:r, 4 * g:4 * g + n, :], ALU.mult, ALU.add).then_inc(c_drained, 1)

            def copy_out(g, par):
                dve.wait_ge(o_stored[par], 16 * ((g - par) // 2) + 16)
                dve.wait_ge(used, UPH * g + UPH - 1 + 4)
                nc.vector.tensor_copy(OB[par][:, 0:512], PO[0][:]).then_inc(o_out[0], 1)
                dve.wait_ge(used, UPH * g + UPH + 4)
                nc.vector.tensor_copy(OB[par][:, 512:OW], PO[1][:, 0:OW - 512]).then_inc(o_out[1], 1)

            for i in range(2):
                nc.vector.memset(KA[i][KR:KS, :], 1.0).then_inc(consts, 1)
            nc.vector.memset(H[:, NT - 1, :], 0.0)
            nc.vector.memset(MX[:], 0.0)
            nc.vector.memset(MV[:], 1.0).then_inc(consts, 1)
            dve.wait_ge(consts, 6)
            dve.wait_ge(bound_step, 4)
            nc.vector.tensor_tensor(bound[:, 0:2], nrm[:], ab[:], ALU.add).then_inc(bound_step, 1)
            dve.wait_ge(bound_step, 5)
            nc.vector.tensor_tensor(bound[:, 2:4], bound[:, 0:2], bound[:, 0:2], ALU.mult).then_inc(bound_step, 1)
            dve.wait_ge(bound_step, 7)
            nc.vector.tensor_copy(hq[:, 0:2 * HEADS], S[0][0:1, 2, 0:2 * HEADS]).then_inc(bound_step, 1)
            dve.wait_ge(bound_step, 8)
            nc.vector.tensor_tensor(hq[:, 2 * HEADS:], hq[:, 0:HEADS], hq[:, HEADS:2 * HEADS],
                                    ALU.mult).then_inc(bound_step, 1)
            dve.wait_ge(bound_step, 9)
            nc.vector.tensor_reduce(hq[:, 0:1], hq[:, 2 * HEADS:], AX.X, ALU.max).then_inc(exp_loaded, 1)
            dve.wait_ge(exp_loaded, 2)
            nc.vector.tensor_scalar(flag[:], hq[:, 0:1], (SAFE / SCALE) ** 2, None, ALU.is_gt).then_inc(bound_step, 1)
            dve.wait_ge(bound_step, 10)
            needed = dve.value_load(flag[0:1, 0:1], min_val=0, max_val=1)
            dve.wait_ge(early_in, 8 * 16)
            for i in range(NA):
                before_job(0, i, S[i % 2][:, 2, :])
            with dve.If(needed > 0):
                maxima_job(0)
            with dve.Fori(0, B) as b:
                ac.begin()
                cc.begin()
                if not cc.per_image:
                    cc.per_image = C_STEPS
                for h in range(HEADS):
                    if h in A_AT:
                        with dve.If(b < B - 1):
                            for kt, i in A_AT[h].items():
                                before_job(following(b), i, S[(h + kt + 1) % 2][:, 2, :])
                            if h == 4:
                                wait_apart(dve, v_stored, 16 * b + 32, passed)
                    if h == MAXIMA_AT[0]:
                        with dve.If(b + (1 - needed) * B < B - 1):
                            maxima_job(following(b))
                        with dve.If(b > 0):
                            attention_job(b)
                    if h in C_AT:
                        with dve.If(b > 0):
                            for kt, i in C_AT[h].items():
                                after_job(b, i, S[(h + kt + 1) % 2][:, 2, :])
                    copy_out(HEADS * b + h, h % 2)
            ac.begin()
            cc.begin()
            assert cc.per_image == C_STEPS
            attention_job(B)
            for i in range(NCP):
                after_job(B, i, S[i % 2][:, 2, :])

        @block.tensor
        def _(pe):
            def before_piece(a, i, bank, half):
                kind, g = A_PIECES[i]
                last = None
                if half == 0 or GROUPS[g][1] == 1:
                    if kind == "embed" and g == 0:
                        pe.wait_ge(pixels_in, 32 * a + 32)
                    elif kind == "turn":
                        pe.wait_ge(xn_ready, NG * a + g + 1)
                    elif kind == "value":
                        pe.wait_ge(a_drained, NA * a + NG + g + 1)
                if kind in ("embed", "turn", "value"):
                    for t in tiles(g, half):
                        r, at = rows_of(t), (t % 4) * C
                        if kind == "embed":
                            last = nc.tensor.matmul(bank[0:r, at:at + C], XS[:, t * P:t * P + r], WE[:],
                                                    start=True, stop=True)
                        elif kind == "turn":
                            last = nc.tensor.transpose(bank[:, at:at + r], XN[0:r, t, :], ident[0:r, 0:r])
                        else:
                            last = nc.tensor.matmul(bank[0:r, at:at + C], XNT[:, t * P:t * P + r], WV[:],
                                                    start=True, stop=True)
                else:
                    side = A_KINDS.index(kind) - 3
                    s, w = CHUNKS[g]
                    w0 = w // 4 * 2
                    x, y = (0, w0) if half == 0 else (w0, w)
                    last = nc.tensor.matmul(bank[:, x:y], WQK[:, side, :], XNT[:, s + x:s + y], start=True, stop=True)
                if half == 1:
                    last.then_inc(a_issued, 1)

            def tiles(g, half):
                g0, n = 4 * g, GROUPS[g][1]
                return range(g0, g0 + n // 2) if half == 0 else range(g0 + n // 2, g0 + n)

            def after_piece(turn, i, bank, half):
                kind, g = C_PIECES[i]
                last = None
                first = half == 0 or GROUPS[g][1] == 1
                if kind == "project":
                    if first and g == 0:
                        pe.wait_ge(attn_ready, turn + 1)
                    for t in tiles(g, half):
                        r, at = rows_of(t), (t % 4) * C
                        last = nc.tensor.matmul(bank[0:r, at:at + C], NUM[:, t * P:t * P + r], WP[:],
                                                start=True, stop=True)
                elif kind == "turn":
                    if first:
                        pe.wait_ge(xn2_ready, NG * turn + g + 1)
                    for t in tiles(g, half):
                        r, at = rows_of(t), (t % 4) * C
                        last = nc.tensor.transpose(bank[:, at:at + r], XN[0:r, t, :], ident[0:r, 0:r])
                elif kind == "route":
                    if half == 1:
                        pe.wait_ge(routed, 4 * turn + 1)
                        last = nc.tensor.matmul(bank[0:1, 0:EXPERTS], mean[:], WG[:], start=True, stop=True)
                elif kind == "gate":
                    if half == 1:
                        pe.wait_ge(routed, 4 * turn + 4)
                        pe.wait_ge(expert_in, 32 * turn + 32)
                        nc.tensor.matmul(bank[:, 0:1], ones[:], gate[:], start=True, stop=True)
                        last = nc.tensor.matmul(bank[:, 4:4 + C], ones[:], BS[:], start=True, stop=True)
                else:
                    for t in tiles(g, half):
                        r, at = rows_of(t), (t % 4) * C
                        last = nc.tensor.matmul(bank[0:r, at:at + C], XNT[:, t * P:t * P + r], WS[:],
                                                start=True, stop=True)
                if half == 1:
                    last.then_inc(c_issued, 1)

            def maxima(a):
                with pe.Fori(0, HEADS) as head:
                    wait_apart(pe, m_loaded, 2 * PAIRS * 16 * (HEADS * a + head + 1), passed)
                    n0 = MPI * a + NT * NMAX * head

                    def tile(t, q, r):
                        for c in range(NMAX):
                            pe.wait_ge(m_reduced, n0 + NMAX * t + c + 1)
                            nc.tensor.matmul(S[1][0:r, 2, 0:WMAX], q, KM[:, MAX_AT[c]:MAX_AT[c] + WMAX],
                                             start=True, stop=True).then_inc(m_scored, 1)

                    with pe.Fori(0, NT - 1) as t:
                        tile(t, KQM[0:KR, ds(t * P + N, P)], P)
                    tile(NT - 1, QM[:, N - LAST:N], LAST)
                wait_apart(pe, m_reduced, MPI * a + MPI + 1, passed)

            def qk(b, h, kt, u, wait=True):
                q0, w, n, _ = UNITS[u]
                par, r = h % 2, rows_of(kt)
                if wait:
                    pe.wait_ge(probs, UPI * b + UPH * h + NU * kt + u - 1)
                for j in range(n):
                    last = nc.tensor.matmul(S[(par + kt + u) % 2][0:r, j, 0:w], KA[par][:, kt * P:kt * P + r],
                                            QA[par][:, q0 + j * w:q0 + (j + 1) * w], start=True, stop=True)
                last.then_inc(scores, 1)

            def pv(b, h, kt, u):
                par, r, pw = h % 2, rows_of(kt), UNITS[u][3]
                bank, at = OFF[u] // 512, OFF[u] % 512
                pe.wait_ge(probs, UPI * b + UPH * h + NU * kt + u + 1)
                if u == 0:
                    pe.wait_ge(v_staged, NT * HEADS * b + NT * h + kt + 2)
                if kt == 0 and u != 1:
                    pe.wait_ge(o_out[bank], HEADS * b + h + 1)
                for j in range(4):
                    last = nc.tensor.matmul(PO[bank][32 * j:32 * j + 32, at:at + pw], VST[(par + kt) % 2][0:r, :],
                                            E[u][0:r, j * pw:(j + 1) * pw], start=kt == 0 and u != 1,
                                            stop=kt == NT - 1, skip_group_check=True)
                last.then_inc(used, 1)

            def first_scores(b, h, u, wait=True):
                if u == 0:
                    pe.wait_ge(qk_in[h % 2], 16 * LOADS * (HEADS // 2 * b + h // 2 + 1))
                qk(b, h, 0, u, wait)

            pe.wait_ge(early_in, 8 * 16)
            pe.wait_ge(consts, 6)
            pe.wait_ge(bound_step, 6)
            nc.tensor.matmul(S[0][0:1, 2, 0:HEADS], bound[:, 2:3], HSUM[:], start=True, stop=True)
            nc.tensor.matmul(S[0][0:1, 2, HEADS:2 * HEADS], bound[:, 3:4], HSUM[:], start=True,
                             stop=True).then_inc(bound_step, 1)
            pe.wait_ge(bound_step, 10)
            needed = pe.value_load(flag[0:1, 0:1], min_val=0, max_val=1)
            for i in range(NA):
                if i >= 2:
                    pe.wait_ge(a_drained, i - 1)
                for half in range(2):
                    before_piece(0, i, S[i % 2][:, 2, :], half)
            with pe.If(needed > 0):
                pe.wait_ge(a_drained, NA)
                maxima(0)
            pe.wait_ge(a_drained, NA)
            pe.wait_ge(weights_in, 6 * 16)
            first_scores(0, 0, 0, wait=False)
            first_scores(0, 0, 1, wait=False)
            with pe.Fori(0, B) as b:
                for h in range(HEADS):
                    a_at, c_at = A_AT.get(h, {}), C_AT.get(h, {})

                    def background(kt, half):
                        bank = S[(h + kt + 1) % 2][:, 2, :]
                        if kt in a_at:
                            with pe.If(b < B - 1):
                                before_piece(following(b), a_at[kt], bank, half)
                        if kt in c_at:
                            with pe.If(b > 0):
                                after_piece(b, c_at[kt], bank, half)
                        if (h, kt) == MAXIMA_AT and half == 1:
                            with pe.If(b + (1 - needed) * B < B - 1):
                                maxima(following(b))

                    def third_bank_free(kt):
                        if kt - 1 in a_at:
                            with pe.If(b < B - 1):
                                pe.wait_ge(a_drained, NA * following(b) + a_at[kt - 1] + 1)
                        if kt - 1 in c_at:
                            with pe.If(b > 0):
                                pe.wait_ge(c_drained, NCP * b + c_at[kt - 1] + 1)

                    qk(b, h, 0, 2)
                    pv(b, h, 0, 0)
                    for kt in range(1, NT):
                        qk(b, h, kt, 0)
                        pv(b, h, kt - 1, 1)
                        qk(b, h, kt, 1)
                        background(kt, 0)
                        pv(b, h, kt - 1, 2)
                        third_bank_free(kt)
                        qk(b, h, kt, 2)
                        background(kt, 1)
                        pv(b, h, kt, 0)
                    for u in range(2):
                        if h < HEADS - 1:
                            first_scores(b, h + 1, u)
                        else:
                            with pe.If(b < B - 1):
                                first_scores(following(b), 0, u)
                        pv(b, h, NT - 1, u + 1)
            for i in range(NCP):
                pe.wait_ge(c_drained, NCP * B + max(i - 1, 0))
                for half in range(2):
                    after_piece(B, i, S[i % 2][:, 2, :], half)


def kernel(x, cls_tok, L0_tok_W, L0_tok_b, L0_tok_cls, L0_attn_Wqkv, L0_attn_bqkv, L0_attn_Wproj, L0_attn_bproj,
           L0_ffn_Wg, L0_ffn_bg, L0_ffn_We, L0_ffn_be):
    import numpy as np
    import concourse.bacc as bacc
    from concourse import mybir as _mybir
    from concourse.bass_utils import run_bass_kernel_spmd

    x, cls_tok, W, b, cls = (np.asarray(a) for a in (x, cls_tok, L0_tok_W, L0_tok_b, L0_tok_cls))
    Wqkv, bqkv, Wproj = (np.asarray(a) for a in (L0_attn_Wqkv, L0_attn_bqkv, L0_attn_Wproj))

    freqs = (1.0 / np.float32(THETA) ** (np.arange(0, HD, 2, dtype=np.float32) / np.float32(HD))).astype(np.float32)
    angles = np.outer(np.arange(N, dtype=np.float32), freqs).astype(np.float32)
    comp = np.arange(C) % HD
    sign = np.where(comp % 2 == 0, -1.0, 1.0).astype(np.float32)[:, None]
    cos = np.ascontiguousarray(np.cos(angles).T[comp // 2])
    sin = np.ascontiguousarray(np.sin(angles).T[comp // 2]) * sign
    indicators = np.zeros((3, N), np.float32)
    indicators[0, 2:] = 1.0
    indicators[1, 0] = 1.0
    indicators[2, 1] = 1.0
    head_sum = np.zeros((C, HEADS), np.float32)
    head_sum[np.arange(C), np.arange(C) // HD] = 1.0

    pixels = np.zeros((B, FEAT, N), np.float32)
    pixels[:, :, 2:] = x.reshape(B, 3, GRID, PATCH, GRID, PATCH).transpose(0, 1, 3, 5, 2, 4).reshape(B, FEAT, NP_)

    Wq, Wk, Wv = Wqkv[0:C], Wqkv[C:2 * C], Wqkv[2 * C:]
    bq, bk, bv = bqkv[0:C, None], bqkv[C:2 * C, None], bqkv[2 * C:]
    arrays = {
        "pixels": pixels,
        "indicators": indicators,
        "w_embed": np.concatenate([b[None], cls_tok[0], cls[0], W.T]),
        "w_qk": np.stack([Wq.T, Wk.T], 1),
        "b_qk": np.concatenate([bq, bk], 1),
        "w_v": Wv.T, "b_v": bv,
        "w_row": np.stack([Wq, Wk], 1),
        "head_sum": head_sum, "cos": cos, "sin": sin, "ident": np.eye(P, dtype=np.float32),
        "w_proj": Wproj.T, "b_proj": np.asarray(L0_attn_bproj),
        "w_gate": np.asarray(L0_ffn_Wg), "b_gate": np.asarray(L0_ffn_bg),
        "w_expert": np.asarray(L0_ffn_We), "b_expert": np.asarray(L0_ffn_be),
    }
    nc = bacc.Bacc("TRN2", target_bir_lowering=False, num_devices=1)
    io, feed = {}, {}
    for name, a in arrays.items():
        feed[f"in_{name}"] = np.ascontiguousarray(a)
        io[name] = nc.dram_tensor(f"in_{name}", a.shape, _mybir.dt.from_np(a.dtype), kind="ExternalInput").ap()
    out = nc.dram_tensor("out_0", (B, N, C), _mybir.dt.float32, kind="ExternalOutput").ap()
    vit_tower(nc, io, out)
    r = run_bass_kernel_spmd(nc, [feed], core_ids=[0])
    return r.results[0]["out_0"]
```
